# Optimizing a Trainium2 kernel written in Bass

```python
import numpy as np
import jax
import jax.numpy as jnp

def _softmax(x, axis=-1):
    return jax.nn.softmax(x, axis=axis)

def _gelu(x):
    return jax.nn.gelu(x, approximate=True)

def _silu(x):
    return jax.nn.silu(x)

def _sigmoid(x):
    return jax.nn.sigmoid(x)

def _layernorm(x, axis=-1, eps=1e-05):
    m = jnp.mean(x, axis=axis, keepdims=True)
    v = jnp.var(x, axis=axis, keepdims=True)
    return (x - m) / jnp.sqrt(v + eps)

def _scatter_add(tgt, idx, src, axis=0):
    return tgt.at[idx].add(src)

def _segment_sum(src, seg, n):
    return jax.ops.segment_sum(src, seg, n)
kernel_name = 'mk_audio_tower_d1_tok_audfeat1024_r4_d3783b'

def setup_inputs(seed: int=0):
    np.random.seed(seed)
    _w = jnp.asarray

    def _rec_inputs():
        import jax
        import jax.numpy as jnp
        _rk = jax.random.key(seed)
        x = -7.10856e-05 + 0.999911 * jax.random.normal(jax.random.fold_in(_rk, 1), (64, 250, 256), jnp.float32)
        return x
    x = _rec_inputs()

    def _L0_tok_setup():
        import math
        import jax, jax.numpy as jnp
        import numpy as np
        K = 4
        POS_DIM = 32

        def _fourier_features(pos, dim):
            half = dim // 2
            freqs = jnp.exp(jnp.linspace(0.0, math.log(1000.0), half)).astype(pos.dtype)
            ang = pos[:, None] * freqs
            return jnp.concatenate([jnp.sin(ang), jnp.cos(ang)], axis=-1)
        key = jax.random.key(seed)
        k1, k2, k3 = jax.random.split(key, 3)
        B, M, D = (8, 2048, 256)
        beat_emb = jax.random.normal(k1, (B, M, D), dtype=jnp.float32)
        W = jax.random.normal(k2, (D, D + POS_DIM), dtype=jnp.float32) * 0.02
        b = jax.random.normal(k3, (D,), dtype=jnp.float32) * 0.02
        return {'beat_emb': beat_emb, 'W': W, 'b': b}
    _L0_tok_all = _L0_tok_setup()
    _L0_tok_in = {k: v for k, v in _L0_tok_all.items() if k in ('W', 'b')}
    del _L0_tok_all

    def _L0_attn_setup():
        import jax, jax.numpy as jnp
        import numpy as np
        NUM_HEADS = 16
        SPARSITY = 0.1
        key = jax.random.key(seed)
        ks = jax.random.split(key, 3)
        B, N, C = (2, 512, 256)
        x = jax.random.normal(ks[0], (B, N, C), dtype=jnp.float32)
        w_qkv = jax.random.normal(ks[1], (C, 3 * C), dtype=jnp.float32) * 0.02
        b_qkv = jnp.zeros((3 * C,), dtype=jnp.float32)
        w_out = jax.random.normal(ks[2], (C, C), dtype=jnp.float32) * 0.02
        b_out = jnp.zeros((C,), dtype=jnp.float32)
        return {'x': x, 'w_qkv': w_qkv, 'b_qkv': b_qkv, 'w_out': w_out, 'b_out': b_out}
    _L0_attn_all = _L0_attn_setup()
    _L0_attn_in = {k: v for k, v in _L0_attn_all.items() if k in ('w_qkv', 'b_qkv', 'w_out', 'b_out')}
    del _L0_attn_all

    def _L0_ffn_setup():
        import jax, jax.numpy as jnp
        import numpy as np
        B, S, D_IN, D_OUT = (16, 1024, 256, 256)
        ACT_BITS = 8
        QB = float(2 ** (ACT_BITS - 1) - 1)
        key = jax.random.key(seed)
        k1, k2, k3 = jax.random.split(key, 3)
        x = jax.random.normal(k1, (B, S, D_IN), dtype=jnp.float32)
        ternary_weight = jax.random.randint(k2, (D_OUT, D_IN), 0, 3, dtype=jnp.int32)
        bias = jax.random.normal(k3, (D_OUT,), dtype=jnp.float32)
        act_scale = (jnp.max(jnp.abs(x)) / QB).astype(jnp.float32)
        return {'x': x, 'ternary_weight': ternary_weight, 'bias': bias, 'act_scale': act_scale}
    _L0_ffn_all = _L0_ffn_setup()
    _L0_ffn_in = {k: v for k, v in _L0_ffn_all.items() if k in ('ternary_weight', 'bias', 'act_scale')}
    del _L0_ffn_all
    return {'x': x, 'L0_tok_W': _L0_tok_in['W'], 'L0_tok_b': _L0_tok_in['b'], 'L0_attn_w_qkv': _L0_attn_in['w_qkv'], 'L0_attn_b_qkv': _L0_attn_in['b_qkv'], 'L0_attn_w_out': _L0_attn_in['w_out'], 'L0_attn_b_out': _L0_attn_in['b_out'], 'L0_ffn_ternary_weight': _L0_ffn_in['ternary_weight'], 'L0_ffn_bias': _L0_ffn_in['bias'], 'L0_ffn_act_scale': _L0_ffn_in['act_scale']}

def reference(x, L0_tok_W, L0_tok_b, L0_attn_w_qkv, L0_attn_b_qkv, L0_attn_w_out, L0_attn_b_out, L0_ffn_ternary_weight, L0_ffn_bias, L0_ffn_act_scale):
    import jax
    import jax.numpy as jnp

    def _L0_tok_ref(beat_emb, W, b):
        import math
        import jax, jax.numpy as jnp
        import numpy as np
        K = 4
        POS_DIM = 32

        def _fourier_features(pos, dim):
            half = dim // 2
            freqs = jnp.exp(jnp.linspace(0.0, math.log(1000.0), half)).astype(pos.dtype)
            ang = pos[:, None] * freqs
            return jnp.concatenate([jnp.sin(ang), jnp.cos(ang)], axis=-1)
        B, M, D = beat_emb.shape
        Mb = (M + K - 1) // K
        pad = Mb * K - M
        x = jnp.pad(beat_emb, ((0, 0), (0, pad), (0, 0))) if pad else beat_emb
        sums = x.reshape(B, Mb, K, D).sum(axis=2)
        counts = jnp.minimum(K, M - jnp.arange(Mb) * K).astype(beat_emb.dtype)
        out = sums / counts[None, :, None]
        idx = jnp.arange(Mb, dtype=beat_emb.dtype)
        pos = jnp.clip(idx / max(1, Mb - 1), 0.0, 1.0)
        ff = _fourier_features(pos, POS_DIM)
        ff = jnp.broadcast_to(ff[None], (B, Mb, POS_DIM))
        h = jnp.concatenate([out, ff], axis=-1)
        return jnp.einsum('bmi,oi->bmo', h, W) + b

    def _L0_attn_ref(x, w_qkv, b_qkv, w_out, b_out):
        import jax, jax.numpy as jnp
        import numpy as np
        NUM_HEADS = 16
        SPARSITY = 0.1
        B, N, C = x.shape
        H = NUM_HEADS
        hd = C // H
        scale = hd ** (-0.5)
        qkv = (x @ w_qkv + b_qkv).reshape(B, N, 3, H, hd).transpose(2, 0, 3, 1, 4)
        q, k, v = (qkv[0], qkv[1], qkv[2])
        scores = jnp.einsum('bhnd,bhmd->bhnm', q, k) * scale
        k_sparse = int(SPARSITY * N)
        if 0 < k_sparse < N:
            _, idx = jax.lax.top_k(scores, k_sparse)
            bi = jnp.arange(B)[:, None, None, None]
            hi = jnp.arange(H)[None, :, None, None]
            ni = jnp.arange(N)[None, None, :, None]
            mask = jnp.zeros_like(scores).at[bi, hi, ni, idx].set(1.0)
            scores = scores * mask - 1000000000.0 * (1.0 - mask)
        attn = jax.nn.softmax(scores, axis=-1)
        out = jnp.einsum('bhnm,bhmd->bhnd', attn, v)
        out = out.transpose(0, 2, 1, 3).reshape(B, N, C)
        return out @ w_out + b_out

    def _L0_ffn_ref(x, ternary_weight, bias, act_scale):
        import jax, jax.numpy as jnp
        import numpy as np
        B, S, D_IN, D_OUT = (16, 1024, 256, 256)
        ACT_BITS = 8
        QB = float(2 ** (ACT_BITS - 1) - 1)
        scale = jnp.maximum(act_scale, 1e-05)
        x_int = jnp.clip(jnp.round(x / scale), -QB, QB)
        x_dq = jnp.nan_to_num(x_int * scale, nan=0.0, posinf=10000.0, neginf=-10000.0)
        w = ternary_weight.astype(jnp.float32) - 1.0
        return jnp.einsum('bsi,oi->bso', x_dq, w) + bias
    h = _L0_tok_ref(x, L0_tok_W, L0_tok_b)
    h = h + _L0_attn_ref(_layernorm(h, axis=-1), L0_attn_w_qkv, L0_attn_b_qkv, L0_attn_w_out, L0_attn_b_out)
    h = h + _L0_ffn_ref(_layernorm(h, axis=-1), L0_ffn_ternary_weight, L0_ffn_bias, L0_ffn_act_scale)
    return h

_drawn_inputs = setup_inputs


def setup_inputs(seed=0):
    import zlib

    import numpy as np

    out = dict(_drawn_inputs(seed))
    spreads = {'L0_attn_b_qkv': (0.0, 0.1), 'L0_attn_b_out': (0.0, 0.1)}
    factors = {}
    for name, (base, spread) in spreads.items():
        noise = np.random.default_rng([zlib.crc32(name.encode()), seed]).standard_normal(out[name].shape)
        drawn = base * np.exp(spread * noise) if base else spread * noise
        out[name] = jnp.asarray(drawn.astype(out[name].dtype))
    for name, factor in factors.items():
        out[name] = (out[name] * factor).astype(out[name].dtype)
    return out
```

```python
from contextlib import ExitStack

import concourse.bass as bass
from concourse import mybir

ALU = mybir.AluOpType
ACT = mybir.ActivationFunctionType
AX = mybir.AxisListType
F32 = mybir.dt.float32
BF16 = mybir.dt.bfloat16
I32 = mybir.dt.int32

P = 128
POOL = 4
POS = 32
HEADS = 16
TOPK_SHARE = 0.1
EPS = 1e-5
ACT_MAX = 127.0
ROUND = 12582912.0
F32_MAX = 3.4028234e38
SETUP_BIASES = 10

C_ID, C_INV, C_EVEN, C_ODD, C_FF = 0, P, P + 1, P + 2, P + 3
C_ALL = C_FF + P


def audio_tower(nc, x, w_tok, b_tok, w_qkv, b_qkv, w_out, b_out, w_ffn, b_ffn, act_scale, consts, out):
    B, M, D = x.shape
    N = out.shape[1]
    T = B // 2
    HD = D // HEADS
    PAIRS = HEADS // 2
    TOP = int(TOPK_SHARE * N)
    CH = D // P
    SCALE = float(HD) ** -0.5
    FULL = N - 1 if M < POOL * N else N
    TAIL = M - POOL * FULL
    ROWS = 4
    U = 4
    LAST_LAG = 3
    FIRST_LOOPED = LAST_LAG + 2
    assert D == 2 * P and N == 63 and 2 * HD == 32 and 0 < TOP < 8 and TAIL > 0 and T % 4 == 0

    with ExitStack() as ctx:
        def sb(name, shape, dt=F32):
            return ctx.enter_context(nc.sbuf_tensor(name, shape, dt))

        def sem(name):
            return ctx.enter_context(nc.semaphore(name))

        cst = sb("cst", [P, C_ALL])
        w_tok_rows = sb("w_tok_rows", [P, CH, D + POS])
        w_tokT = sb("w_tokT", [P, CH, D])
        w_posT = sb("w_posT", [POS, D])
        wqkv = sb("wqkv", [P, CH, 3 * D])
        wo = sb("wo", [P, CH, D])
        tern_i = sb("tern_i", [P, CH, D], I32)
        tern_f = sb("tern_f", [P, CH, D])
        ternT = sb("ternT", [P, CH, D], BF16)
        rows = sb("rows", [1, 3 * D + 1])
        bqk = sb("bqk", [P, 2, CH])
        bv = sb("bv", [P, CH])
        bv_wide = sb("bv_wide", [P, CH, P])
        bk_par = sb("bk_par", [P, CH, 2])
        ones = sb("ones", [P, P])
        pos_bias = sb("pos_bias", [P, D])
        attn_bias = sb("attn_bias", [P, D])
        ffn_bias = sb("ffn_bias", [P, D])
        scl = sb("scl", [P, 8])
        ident = cst[:, C_ID:C_ID + P]
        X = sb("X", [P, 2, POOL * D])
        half_sum = sb("half_sum", [P, 2 * D])
        xs = sb("xs", [P, 2, D])
        xsT = sb("xsT", [P, 2, CH, P])
        h = sb("h", [P, 2, D])
        hb = sb("hb", [P, 4, D])
        st1 = sb("st1", [P, 2, 6])
        mv1 = sb("mv1", [P, 2, 2])
        rstd1 = sb("rstd1", [P, 2])
        hn = sb("hn", [P, 2, D])
        hnT = sb("hnT", [P, 2, CH, P])
        q = sb("q", [P, 2, CH, P])
        k = sb("k", [P, 2, CH, 2, 2, 64])
        v = sb("v", [P, 4, 2, PAIRS, 2, HD])
        s = sb("s", [P, 2, HEADS, 64])
        top8 = sb("top8", [P, 2, HEADS, 8])
        etop = sb("etop", [P, 2, HEADS, TOP])
        den = sb("den", [P, 2, HEADS])
        lden = sb("lden", [P, 2, HEADS])
        shift = sb("shift", [P, 2, HEADS])
        e = sb("e", [P, 2, HEADS, 64])
        mask = sb("mask", [P, 2, HEADS, 64])
        pr = sb("pr", [P, 2, HEADS, 64])
        prT = sb("prT", [P, 2, PAIRS, P])
        oT = sb("oT", [P, 2, CH, P])
        h2 = sb("h2", [P, 2, D])
        h2b = sb("h2b", [P, 2, D])
        st2 = sb("st2", [P, 2, 6])
        mv2 = sb("mv2", [P, 2, 2])
        rstd2 = sb("rstd2", [P, 2])
        rq = sb("rq", [P, 2])
        qf = sb("qf", [P, 2, D])
        xi = sb("xi", [P, 2, D])
        xiT = sb("xiT", [P, 2, CH, P], BF16)
        y = sb("y", [P, 2, D])
        var_eps = sb("var_eps", [P, 2, 2])
        expo = sb("expo", [P, 1])

        psS = ctx.enter_context(nc.psum_tensor("psS", [P, ROWS, 512], F32))
        psQK = ctx.enter_context(nc.psum_tensor("psQK", [P, 4, P], F32))
        psB = ctx.enter_context(nc.psum_tensor("psB", [P, 3, 512], F32))
        ps_s = psS[:, :, 0:256]
        psT = psS[:, 0:2, :].rearrange("p b (j n) -> p (b j) n", n=P)
        ps_ff = psS[:, 2, 0:256]
        ps_v, ps_oT = psB[:, 0, 0:256], psB[:, 0, 256:512]
        ps_x, ps_n = psB[:, 1, 0:256], psB[:, 1, 256:512]
        ps_h, ps_ao = psB[:, 2, 0:256], psB[:, 2, 256:512]

        consts_in = sem("consts_in")
        tok_w_in = sem("tok_w_in")
        qkv_w_in = sem("qkv_w_in")
        out_w_in = sem("out_w_in")
        ffn_w_in = sem("ffn_w_in")
        rows_in = sem("rows_in")
        bias_in = sem("bias_in")
        cleared = sem("cleared")
        ones_set = sem("ones_set")
        zeroed = sem("zeroed")
        setup_ps = sem("setup_ps")
        setup_sb = sem("setup_sb")
        setup_dve = sem("setup_dve")
        x_in = [sem(f"x_in{i}") for i in range(2)]
        half_done = sem("half_done")
        xs_done = sem("xs_done")
        xsT_ps = sem("xsT_ps")
        xsT_done = sem("xsT_done")
        h_ps = sem("h_ps")
        h_done = sem("h_done")
        st1_done = sem("st1_done")
        mv1_done = sem("mv1_done")
        ve1_done = sem("ve1_done")
        rstd1_done = sem("rstd1_done")
        hb_done = sem("hb_done")
        hn_done = sem("hn_done")
        hnT_ps = sem("hnT_ps")
        hnT_done = sem("hnT_done")
        qk_ps = sem("qk_ps")
        v_ps = sem("v_ps")
        qk_done = sem("qk_done")
        v_done = sem("v_done")
        s_ps = sem("s_ps")
        s_done = sem("s_done")
        top8_done = sem("top8_done")
        ztop_done = sem("ztop_done")
        etop_done = sem("etop_done")
        den_done = sem("den_done")
        lden_done = sem("lden_done")
        shift_done = sem("shift_done")
        mask_done = sem("mask_done")
        z_done = sem("z_done")
        e_done = sem("e_done")
        p_done = sem("p_done")
        pT_ps = sem("pT_ps")
        pT_done = sem("pT_done")
        oT_ps = sem("oT_ps")
        oT_done = sem("oT_done")
        ao_ps = sem("ao_ps")
        h2_done = sem("h2_done")
        st2_done = sem("st2_done")
        mv2_done = sem("mv2_done")
        ve2_done = sem("ve2_done")
        rstd2_done = sem("rstd2_done")
        h2b_done = sem("h2b_done")
        rq_done = sem("rq_done")
        qf_done = sem("qf_done")
        xi_done = sem("xi_done")
        xiT_ps = sem("xiT_ps")
        xiT_done = sem("xiT_done")
        ff_ps = sem("ff_ps")
        y_done = sem("y_done")
        y_out = [sem(f"y_out{i}") for i in range(2)]

        x_full = x[:, 0:POOL * FULL, :].rearrange("(t b) (p f) i -> t b p (f i)", b=2, f=POOL)
        x_tail = x[:, POOL * FULL:M, :].rearrange("(t b) f i -> t b (f i)", b=2)
        out_t = out.rearrange("(t b) n o -> t b n o", b=2)

        class Tile:

            def __init__(self, u, c):
                self.u, self.c = u, c

            def plus(self, d):
                return Tile(self.u, self.c + d)

            def exists(self):
                return not isinstance(self.u, int) or 0 <= U * self.u + self.c < T

            def has(self, back):
                return (self.c if not isinstance(self.u, int) else U * self.u + self.c) >= back

            def index(self):
                return self.u * U + self.c

            def count(self, back=0, per=1, less=0):
                return self.u * (U * per) + ((self.c - back + 1) * per - less)

            def uses(self, back, per):
                return self.u * (U // 2 * per) + ((self.c - back) // 2 + 1) * per

        def run_steps(eng, stages):
            ahead = max(d for d, _ in stages)
            trips = (T - ahead - FIRST_LOOPED) // U

            def step(n):
                for d, stage in stages:
                    if n.plus(d).exists():
                        stage(n.plus(d))

            for n in range(-ahead, FIRST_LOOPED):
                step(Tile(0, n))
            with eng.Fori(0, trips) as u:
                for n in range(U):
                    step(Tile(u, FIRST_LOOPED + n))
            for n in range(FIRST_LOOPED + trips * U, T + LAST_LAG):
                step(Tile(0, n))

        block = ctx.enter_context(nc.Block())

        @block.sync
        def _(sp):
            def load(t):
                slot = t.c % 2
                if t.has(2):
                    sp.wait_ge(xs_done, t.count(2))
                else:
                    sp.wait_ge(cleared, 1)
                for b in range(2):
                    sp.dma_start(X[64 * b:64 * b + FULL, slot, :], x_full[t.index(), b])\
                        .then_inc(x_in[slot], 16)
                sp.dma_start(X[FULL:P:64, slot, 0:TAIL * D], x_tail[t.index()]).then_inc(x_in[slot], 16)

            def store(t):
                slot = t.c % 2
                sp.wait_ge(y_done, t.count())
                for b in range(2):
                    sp.dma_start(out_t[t.index(), b], y[64 * b:64 * b + N, slot, :])\
                        .then_inc(y_out[slot], 16)

            run_steps(sp, [(4, load), (-3, store)])
            for slot in range(2):
                sp.wait_ge(y_out[slot], 2 * 16 * (T // 2))

        @block.gpsimd
        def _(pool):
            nc.gpsimd.memset(X[:, :, :], 0.0).then_inc(cleared, 1)
            nc.gpsimd.memset(expo[:, :], -0.5).then_inc(zeroed, 1)
            nc.gpsimd.memset(v[:, :, :, :, :, :], 0.0).then_inc(zeroed, 1)
            nc.gpsimd.memset(pr[:, :, :, :], 0.0).then_inc(zeroed, 1)
            pool.wait_ge(zeroed, 3)

            def pool_frames(t):
                slot = t.c % 2
                pool.wait_ge(x_in[slot], t.uses(0, 48))
                nc.gpsimd.tensor_tensor(half_sum[:, :], X[:, slot, 0:2 * D], X[:, slot, 2 * D:4 * D],
                                        ALU.add).then_inc(half_done, 1)
                if t.has(2):
                    pool.wait_ge(xsT_ps, t.count(2))
                pool.wait_ge(half_done, t.count())
                nc.gpsimd.tensor_tensor(xs[:, slot, :], half_sum[:, 0:D], half_sum[:, D:2 * D],
                                        ALU.add).then_inc(xs_done, 1)

            def rstd_1(t):
                slot = t.c % 2
                pool.wait_ge(ve1_done, t.count())
                if t.has(2):
                    pool.wait_ge(hn_done, t.count(2))
                nc.gpsimd.tensor_tensor(rstd1[:, slot:slot + 1], var_eps[:, slot, 0:1], expo[:, :],
                                        ALU.pow).then_inc(rstd1_done, 1)

            def residual_1(t):
                if t.c == 0 and isinstance(t.u, int):
                    pool.wait_ge(setup_dve, SETUP_BIASES)
                pool.wait_ge(h_done, t.count())
                if t.has(4):
                    pool.wait_ge(h2_done, t.count(4))
                nc.gpsimd.tensor_tensor(hb[:, t.c % 4, :], h[:, t.c % 2, :], attn_bias[:, :],
                                        ALU.add).then_inc(hb_done, 1)

            def subtract_shift(t):
                slot = t.c % 2
                pool.wait_ge(shift_done, t.count())
                pool.wait_ge(s_done, t.count())
                if t.has(2):
                    pool.wait_ge(p_done, t.count(2))
                nc.gpsimd.tensor_tensor(
                    e[:, slot, :, 0:N], s[:, slot, :, 0:N],
                    shift[:, slot, :].unsqueeze(2).broadcast_to([P, HEADS, N]),
                    ALU.subtract).then_inc(z_done, 1)

            def keep_top(t):
                slot = t.c % 2
                pool.wait_ge(e_done, t.count())
                pool.wait_ge(mask_done, t.count())
                if t.has(2):
                    pool.wait_ge(pT_ps, t.count(2, per=2))
                nc.gpsimd.tensor_tensor(pr[:, slot, :, 0:N], e[:, slot, :, 0:N], mask[:, slot, :, 0:N],
                                        ALU.mult).then_inc(p_done, 1)

            def rstd_2(t):
                slot = t.c % 2
                pool.wait_ge(ve2_done, t.count())
                if t.has(2):
                    pool.wait_ge(rq_done, t.count(2))
                nc.gpsimd.tensor_tensor(rstd2[:, slot:slot + 1], var_eps[:, slot, 1:2], expo[:, :],
                                        ALU.pow).then_inc(rstd2_done, 1)

            def residual_2(t):
                slot = t.c % 2
                pool.wait_ge(h2_done, t.count())
                if t.has(2):
                    pool.wait_ge(y_done, t.count(2))
                nc.gpsimd.tensor_tensor(h2b[:, slot, :], h2[:, slot, :], ffn_bias[:, :],
                                        ALU.add).then_inc(h2b_done, 1)

            run_steps(pool, [(-1, subtract_shift), (1, rstd_1), (1, residual_1), (2, pool_frames),
                             (-2, rstd_2), (-2, residual_2), (-1, keep_top)])

        @block.scalar
        def _(act):
            act.wait_ge(cleared, 1)
            act.dma_start(cst[:, :], consts).then_inc(consts_in, 16)
            act.dma_start(w_tok_rows[:, :, :], w_tok.rearrange("(c p) i -> p c i", p=P)).then_inc(tok_w_in, 16)
            act.dma_start(rows[0:1, 0:D], b_tok).then_inc(rows_in, 16)
            act.dma_start(rows[0:1, D:2 * D], b_out).then_inc(rows_in, 16)
            act.dma_start(rows[0:1, 2 * D:3 * D], b_ffn).then_inc(rows_in, 16)
            act.dma_start(rows[0:1, 3 * D:3 * D + 1], act_scale).then_inc(rows_in, 16)
            act.dma_start(wqkv[:, :, :], w_qkv.rearrange("(c p) o -> p c o", p=P)).then_inc(qkv_w_in, 16)
            b_cols = b_qkv.rearrange("(j c p) -> j p c", c=CH, p=P)
            for j in range(2):
                act.dma_start(bqk[:, j, :], b_cols[j], allow_slow_non_contiguous=True).then_inc(bias_in, 16)
            act.dma_start(bv[:, :], b_cols[2], allow_slow_non_contiguous=True).then_inc(bias_in, 16)
            act.dma_start(wo[:, :, :], w_out.rearrange("(c p) o -> p c o", p=P)).then_inc(out_w_in, 16)
            act.dma_start(tern_i[:, :, :], w_ffn.rearrange("(c p) i -> p c i", p=P)).then_inc(ffn_w_in, 16)
            act.wait_ge(bias_in, 48)
            act.wait_ge(consts_in, 16)
            for c in range(CH):
                for par in range(2):
                    nc.scalar.activation(bk_par[:, c, par:par + 1], bqk[:, 1, c:c + 1], ACT.Copy,
                                         scale=cst[:, C_EVEN + par:C_EVEN + par + 1]).then_inc(setup_sb, 1)
            act.wait_ge(setup_sb, 2 * CH)

            def copy_xsT(t):
                slot = t.c % 2
                act.wait_ge(xsT_ps, t.count())
                if t.has(2):
                    act.wait_ge(h_ps, t.count(2))
                nc.scalar.activation(xsT[:, slot, :, :], ps_x.rearrange("p (c n) -> p c n", c=CH),
                                     ACT.Copy).then_inc(xsT_done, 1)

            def copy_hnT(t):
                slot = t.c % 2
                act.wait_ge(hnT_ps, t.count())
                if t.has(2):
                    act.wait_ge(v_ps, t.count(2))
                nc.scalar.activation(hnT[:, slot, :, :], ps_n.rearrange("p (c n) -> p c n", c=CH),
                                     ACT.Copy).then_inc(hnT_done, 1)

            def bias_qk(t):
                slot = t.c % 2
                act.wait_ge(qk_ps, t.count())
                if t.has(2):
                    act.wait_ge(s_ps, t.count(2))
                for c in range(CH):
                    nc.scalar.activation(q[:, slot, c, :], psQK[:, c, :], ACT.Identity,
                                         bias=bqk[:, 0, c:c + 1])
                for c in range(CH):
                    for par in range(2):
                        last = nc.scalar.activation(
                            k[:, slot, c, :, par, :], psQK[:, CH + c, :].rearrange("p (b n) -> p b n", b=2),
                            ACT.Identity, bias=bk_par[:, c, par:par + 1],
                            scale=cst[:, C_EVEN + par:C_EVEN + par + 1])
                last.then_inc(qk_done, 1)

            def copy_v(t):
                slot = t.c % 4
                act.wait_ge(v_ps, t.count())
                if t.has(4):
                    act.wait_ge(oT_ps, t.count(4))
                for par in range(2):
                    last = nc.scalar.activation(
                        v[64 * par:64 * par + 64, slot, :, :, par, :].rearrange("p b j d -> p (b j) d"),
                        ps_v[64 * par:64 * par + 64, :].rearrange("p (j d) -> p j d", d=HD), ACT.Copy)
                last.then_inc(v_done, 1)

            def copy_s(t):
                slot = t.c % 2
                act.wait_ge(s_ps, t.count())
                if t.has(2):
                    act.wait_ge(z_done, t.count(2))
                    act.wait_ge(mask_done, t.count(2))
                nc.scalar.activation(s[:, slot, :, :].rearrange("p (r g) n -> p r (g n)", r=ROWS), ps_s,
                                     ACT.Copy).then_inc(s_done, 1)

            def exp_top(t):
                slot = t.c % 2
                act.wait_ge(ztop_done, t.count())
                nc.scalar.activation(etop[:, slot, :, :], etop[:, slot, :, :], ACT.Exp,
                                     scale=SCALE).then_inc(etop_done, 1)

            def log_den(t):
                slot = t.c % 2
                act.wait_ge(den_done, t.count())
                if t.has(2):
                    act.wait_ge(shift_done, t.count(2))
                nc.scalar.activation(lden[:, slot, :], den[:, slot, :], ACT.Ln).then_inc(lden_done, 1)

            def exp_all(t):
                slot = t.c % 2
                act.wait_ge(z_done, t.count())
                nc.scalar.activation(e[:, slot, :, 0:N], e[:, slot, :, 0:N], ACT.Exp,
                                     scale=SCALE).then_inc(e_done, 1)

            def copy_pT(t):
                slot = t.c % 2
                if t.has(2):
                    act.wait_ge(oT_ps, t.count(2))
                for i in range(2):
                    act.wait_ge(pT_ps, t.count(per=2, less=1 - i))
                    nc.scalar.activation(prT[:, slot, 4 * i:4 * i + 4, :], psT[:, 4 * i:4 * i + 4, :],
                                         ACT.Copy).then_inc(pT_done, 1)

            def copy_oT(t):
                slot = t.c % 2
                act.wait_ge(oT_ps, t.count())
                if t.has(2):
                    act.wait_ge(ao_ps, t.count(2))
                nc.scalar.activation(oT[:, slot, :, :], ps_oT.rearrange("p (c n) -> p c n", c=CH),
                                     ACT.Copy).then_inc(oT_done, 1)

            act.wait_ge(zeroed, 3)
            run_steps(act, [(0, bias_qk), (1, copy_xsT), (-1, log_den), (0, copy_v), (-2, copy_pT),
                            (-1, exp_all), (0, copy_s), (-2, copy_oT), (1, copy_hnT), (0, exp_top)])

        @block.vector
        def _(dve):
            nc.vector.memset(ones[:, :], 1.0).then_inc(ones_set, 1)
            dve.wait_ge(ones_set, 1)
            dve.wait_ge(ffn_w_in, 16)
            nc.vector.tensor_scalar(tern_f[:, :, :], tern_i[:, :, :], -1.0, None, ALU.add).then_inc(setup_dve, 1)
            dve.wait_ge(bias_in, 48)
            for c in range(CH):
                nc.vector.tensor_scalar(bv_wide[:, c, :], ones[:, :], bv[:, c:c + 1], None,
                                        ALU.mult).then_inc(setup_dve, 1)
            dve.wait_ge(setup_ps, 1)
            nc.vector.tensor_copy(w_tokT[:, :, :], psQK[:, :, :].rearrange("p (c a) n -> p c (a n)", c=CH))\
                .then_inc(setup_dve, 1)
            nc.vector.tensor_copy(w_posT[:, :], ps_oT[0:POS, :]).then_inc(setup_dve, 1)
            dve.wait_ge(setup_ps, 2)
            nc.vector.tensor_copy(pos_bias[:, :], ps_ao).then_inc(setup_dve, 1)
            dve.wait_ge(setup_ps, 3)
            nc.vector.tensor_copy(attn_bias[:, :], ps_n).then_inc(setup_dve, 1)
            nc.vector.tensor_copy(ffn_bias[:, :], ps_v).then_inc(setup_dve, 1)
            nc.vector.tensor_copy(scl[:, 0:1], psT[:, 0, 0:1]).then_inc(setup_dve, 1)
            nc.vector.tensor_copy(ternT[:, :, :], psT[:, 4:8, :].rearrange("p (c a) n -> p c (a n)", c=CH))\
                .then_inc(setup_dve, 1)
            dve.wait_ge(setup_dve, SETUP_BIASES)
            nc.vector.tensor_scalar(scl[:, 1:2], scl[:, 0:1], EPS, F32_MAX, ALU.max, ALU.min).then_inc(setup_dve, 1)
            nc.vector.tensor_tensor(scl[:, 2:3], scl[:, 0:1], scl[:, 0:1], ALU.is_equal).then_inc(setup_dve, 1)
            dve.wait_ge(setup_dve, SETUP_BIASES + 2)
            nc.vector.reciprocal(scl[:, 3:4], scl[:, 1:2]).then_inc(setup_dve, 1)
            nc.vector.tensor_tensor(scl[:, 4:5], scl[:, 1:2], scl[:, 2:3], ALU.mult).then_inc(setup_dve, 1)
            dve.wait_ge(setup_dve, SETUP_BIASES + 4)
            inv_scale, scale_back = scl[:, 3:4], scl[:, 4:5]

            def sum_top(t):
                slot = t.c % 2
                dve.wait_ge(etop_done, t.count())
                if t.has(2):
                    dve.wait_ge(lden_done, t.count(2))
                nc.vector.tensor_reduce(den[:, slot, :], etop[:, slot, :, :], AX.X, ALU.add)\
                    .then_inc(den_done, 1)

            def make_shift(t):
                slot = t.c % 2
                dve.wait_ge(lden_done, t.count())
                if t.has(2):
                    dve.wait_ge(z_done, t.count(2))
                nc.vector.scalar_tensor_tensor(
                    out=shift[:, slot, :], in0=lden[:, slot, :], scalar=1.0 / SCALE,
                    in1=top8[:, slot, :, 0], op0=ALU.mult, op1=ALU.add).then_inc(shift_done, 1)

            def mask_top(t):
                slot = t.c % 2
                dve.wait_ge(s_done, t.count())
                dve.wait_ge(top8_done, t.count())
                if t.has(2):
                    dve.wait_ge(p_done, t.count(2))
                nc.vector.tensor_tensor(
                    mask[:, slot, :, 0:N], s[:, slot, :, 0:N],
                    top8[:, slot, :, TOP - 1:TOP].broadcast_to([P, HEADS, N]),
                    ALU.is_ge).then_inc(mask_done, 1)

            def tokens(t):
                slot = t.c % 2
                dve.wait_ge(h_ps, t.count())
                if t.has(2):
                    dve.wait_ge(hb_done, t.count(2))
                nc.vector.scalar_tensor_tensor(
                    out=h[:, slot, :], in0=ps_h, scalar=cst[:, C_INV:C_INV + 1], in1=pos_bias[:, :],
                    op0=ALU.mult, op1=ALU.add).then_inc(h_done, 1)
                dve.wait_ge(h_done, t.count())
                nc.vector.bn_stats(out=st1[:, slot, :], in_=h[:, slot, :]).then_inc(st1_done, 1)

            def moments_1(t):
                slot = t.c % 2
                dve.wait_ge(st1_done, t.count())
                dve.nop(nofuse=True)
                nc.vector.bn_aggr(out=mv1[:, slot, :], in_=st1[:, slot, :]).then_inc(mv1_done, 1)
                dve.wait_ge(mv1_done, t.count())
                if t.has(2):
                    dve.wait_ge(rstd1_done, t.count(2))
                nc.vector.tensor_scalar(var_eps[:, slot, 0:1], mv1[:, slot, 1:2], EPS, None,
                                        ALU.add).then_inc(ve1_done, 1)

            def normalise(t):
                slot = t.c % 2
                dve.wait_ge(rstd1_done, t.count())
                if t.has(2):
                    dve.wait_ge(hnT_ps, t.count(2))
                nc.vector.tensor_scalar(hn[:, slot, :], h[:, slot, :], mv1[:, slot, 0:1],
                                        rstd1[:, slot:slot + 1], ALU.subtract, ALU.mult).then_inc(hn_done, 1)

            def attended(t):
                slot = t.c % 2
                dve.wait_ge(ao_ps, t.count())
                dve.wait_ge(hb_done, t.count())
                if t.has(2):
                    dve.wait_ge(h2b_done, t.count(2))
                nc.vector.tensor_tensor(h2[:, slot, :], ps_ao, hb[:, t.c % 4, :], ALU.add)\
                    .then_inc(h2_done, 1)
                dve.wait_ge(h2_done, t.count())
                nc.vector.bn_stats(out=st2[:, slot, :], in_=h2[:, slot, :]).then_inc(st2_done, 1)

            def moments_2(t):
                slot = t.c % 2
                dve.wait_ge(st2_done, t.count())
                dve.nop(nofuse=True)
                nc.vector.bn_aggr(out=mv2[:, slot, :], in_=st2[:, slot, :]).then_inc(mv2_done, 1)
                dve.wait_ge(mv2_done, t.count())
                if t.has(2):
                    dve.wait_ge(rstd2_done, t.count(2))
                nc.vector.tensor_scalar(var_eps[:, slot, 1:2], mv2[:, slot, 1:2], EPS, None,
                                        ALU.add).then_inc(ve2_done, 1)

            def quant_scale(t):
                slot = t.c % 2
                dve.wait_ge(rstd2_done, t.count())
                nc.vector.tensor_tensor(rq[:, slot:slot + 1], rstd2[:, slot:slot + 1], inv_scale,
                                        ALU.mult).then_inc(rq_done, 1)

            def scaled(t):
                slot = t.c % 2
                dve.wait_ge(rq_done, t.count())
                nc.vector.tensor_scalar(qf[:, slot, :], h2[:, slot, :], mv2[:, slot, 0:1],
                                        rq[:, slot:slot + 1], ALU.subtract, ALU.mult).then_inc(qf_done, 1)

            def rounded(t):
                slot = t.c % 2
                dve.wait_ge(qf_done, t.count())
                if t.has(2):
                    dve.wait_ge(xiT_ps, t.count(2))
                nc.vector.tensor_scalar(xi[:, slot, :], qf[:, slot, :], ACT_MAX, ROUND, ALU.min, ALU.add)\
                    .then_inc(xi_done, 1)

            def integers(t):
                slot = t.c % 2
                dve.wait_ge(xiT_ps, t.count())
                if t.has(2):
                    dve.wait_ge(ff_ps, t.count(2))
                nc.vector.tensor_scalar(xiT[:, slot, :, :], ps_x.rearrange("p (c n) -> p c n", c=CH),
                                        ROUND - ACT_MAX, ROUND, ALU.max, ALU.subtract).then_inc(xiT_done, 1)

            def top_scores(t):
                slot = t.c % 2
                dve.wait_ge(s_done, t.count())
                if t.has(2):
                    dve.wait_ge(shift_done, t.count(2))
                    dve.wait_ge(mask_done, t.count(2))
                dve.nop(nofuse=True)
                for g in range(HEADS):
                    last = nc.vector.max(out=top8[:, slot, g, :], in_=s[:, slot, g, 0:N])
                last.then_inc(top8_done, 1)

            def shift_top(t):
                slot = t.c % 2
                dve.wait_ge(top8_done, t.count())
                if t.has(2):
                    dve.wait_ge(den_done, t.count(2))
                nc.vector.tensor_tensor(
                    etop[:, slot, :, :], top8[:, slot, :, 0:TOP],
                    top8[:, slot, :, 0:1].broadcast_to([P, HEADS, TOP]),
                    ALU.subtract).then_inc(ztop_done, 1)

            def finished(t):
                slot = t.c % 2
                dve.wait_ge(ff_ps, t.count())
                dve.wait_ge(h2b_done, t.count())
                if t.has(2):
                    dve.wait_ge(y_out[slot], t.uses(2, 32))
                nc.vector.scalar_tensor_tensor(
                    out=y[:, slot, :], in0=ps_ff, scalar=scale_back, in1=h2b[:, slot, :],
                    op0=ALU.mult, op1=ALU.add).then_inc(y_done, 1)

            run_steps(dve, [(-1, sum_top), (-3, quant_scale), (-3, scaled), (-1, make_shift), (-3, rounded),
                            (1, tokens), (1, moments_1), (-1, mask_top), (1, normalise),
                            (-2, attended), (-2, moments_2), (-3, integers), (0, top_scores),
                            (0, shift_top), (-3, finished)])

        @block.tensor
        def _(pe):
            pe.wait_ge(consts_in, 16)
            pe.wait_ge(tok_w_in, 16)
            for c in range(CH):
                for o in range(CH):
                    nc.tensor.transpose(psQK[:, 2 * c + o, :], w_tok_rows[:, o, c * P:(c + 1) * P], ident)
            for o in range(CH):
                last = nc.tensor.transpose(ps_oT[0:POS, o * P:(o + 1) * P], w_tok_rows[:, o, D:D + POS], ident)
            last.then_inc(setup_ps, 1)
            pe.wait_ge(ones_set, 1)
            pe.wait_ge(rows_in, 64)
            pe.wait_ge(setup_dve, 5)
            nc.tensor.matmul(ps_ao, cst[0:POS, C_FF:C_FF + P], w_posT[:, :], start=True, stop=False)
            nc.tensor.matmul(ps_ao, ones[0:1, :], rows[0:1, 0:D], start=False, stop=True).then_inc(setup_ps, 1)
            pe.wait_ge(out_w_in, 16)
            for c in range(CH):
                nc.tensor.matmul(ps_n, bv_wide[:, c, :], wo[:, c, :], start=(c == 0), stop=False)
            nc.tensor.matmul(ps_n, ones[0:1, :], rows[0:1, D:2 * D], start=False, stop=True)
            nc.tensor.matmul(ps_v, ones[0:1, :], rows[0:1, 2 * D:3 * D], start=True, stop=True)
            nc.tensor.matmul(psT[:, 0, 0:1], ones[0:1, :], rows[0:1, 3 * D:3 * D + 1], start=True, stop=True)
            for c in range(CH):
                for o in range(CH):
                    last = nc.tensor.transpose(psT[:, 4 + 2 * c + o, :], tern_f[:, o, c * P:(c + 1) * P], ident)
            last.then_inc(setup_ps, 1)
            pe.wait_ge(qkv_w_in, 16)
            pe.wait_ge(setup_dve, SETUP_BIASES)

            def transpose_xs(t):
                pe.wait_ge(xs_done, t.count())
                for c in range(CH):
                    last = nc.tensor.transpose(ps_x[:, c * P:(c + 1) * P], xs[:, t.c % 2, c * P:(c + 1) * P],
                                               ident)
                last.then_inc(xsT_ps, 1)

            def token_products(t):
                pe.wait_ge(xsT_done, t.count())
                if t.has(4):
                    pe.wait_ge(h2_done, t.count(4))
                for c in range(CH):
                    last = nc.tensor.matmul(ps_h, xsT[:, t.c % 2, c, :], w_tokT[:, c, :],
                                            start=(c == 0), stop=(c == CH - 1))
                last.then_inc(h_ps, 1)

            def transpose_hn(t):
                pe.wait_ge(hn_done, t.count())
                for c in range(CH):
                    last = nc.tensor.transpose(ps_n[:, c * P:(c + 1) * P], hn[:, t.c % 2, c * P:(c + 1) * P],
                                               ident)
                last.then_inc(hnT_ps, 1)

            def qkv(t):
                slot = t.c % 2
                pe.wait_ge(hnT_done, t.count())
                for o in range(2 * CH):
                    for c in range(CH):
                        last = nc.tensor.matmul(psQK[:, o, :], wqkv[:, c, o * P:(o + 1) * P],
                                                hnT[:, slot, c, :], start=(c == 0), stop=(c == CH - 1))
                last.then_inc(qk_ps, 1)
                if t.has(1):
                    pe.wait_ge(v_done, t.count(1))
                for b in range(2):
                    for c in range(CH):
                        for par in range(2):
                            w = wqkv[:, c, 2 * D:3 * D].rearrange("p (j a d) -> p a j d", a=2, d=HD)[:, par]
                            last = nc.tensor.matmul(
                                ps_v[64 * par:64 * par + 64, b * P:(b + 1) * P],
                                hnT[:, slot, c, 64 * b:64 * b + 64], w, start=(c == 0), stop=(c == CH - 1))
                last.then_inc(v_ps, 1)

            def scores(t):
                slot = t.c % 2
                pe.wait_ge(qk_done, t.count())
                if t.has(1):
                    pe.wait_ge(s_done, t.count(1))
                if t.has(2):
                    pe.wait_ge(pT_done, t.count(2, per=2))
                if t.has(4):
                    pe.wait_ge(y_done, t.count(4))
                for c in range(CH):
                    for r in range(ROWS):
                        at = slice(32 * r, 32 * r + 32)
                        for b in range(2):
                            last = nc.tensor.matmul(
                                ps_s[64 * b:64 * b + 64, r, c * P:(c + 1) * P],
                                q[at, slot, c, 64 * b:64 * b + 64],
                                k[at, slot, c, b, :, :].rearrange("p a n -> p (a n)"), start=True, stop=True)
                last.then_inc(s_ps, 1)

            def transpose_p(t):
                pe.wait_ge(p_done, t.count())
                if t.plus(1).exists():
                    pe.wait_ge(s_done, t.count(-1))
                for i in range(2):
                    for j in range(4 * i, 4 * i + 4):
                        last = nc.tensor.transpose(
                            psT[:, j, :], pr[:, t.c % 2, 2 * j:2 * j + 2, :].rearrange("p a n -> p (a n)"), ident)
                    last.then_inc(pT_ps, 1)

            def weigh_v(t):
                slot = t.c % 2
                ahead = 2 if t.plus(2).exists() else 1 if t.plus(1).exists() else 0
                pe.wait_ge(v_done, t.count(-ahead))
                pe.wait_ge(pT_done, t.count(per=2))
                for c in range(CH):
                    for b in range(2):
                        for r in range(ROWS):
                            last = nc.tensor.matmul(
                                ps_oT[32 * r:32 * r + 32, c * P + 64 * b:c * P + 64 * b + 64],
                                v[:, t.c % 4, b, ROWS * c + r, :, :].rearrange("p a d -> p (a d)"),
                                prT[:, slot, 2 * r + c, 64 * b:64 * b + 64], start=True, stop=True)
                last.then_inc(oT_ps, 1)

            def project(t):
                pe.wait_ge(oT_done, t.count())
                if t.has(1):
                    pe.wait_ge(h2_done, t.count(1))
                if t.plus(3).exists():
                    pe.wait_ge(h_done, t.count(-3))
                for c in range(CH):
                    last = nc.tensor.matmul(ps_ao, oT[:, t.c % 2, c, :], wo[:, c, :],
                                            start=(c == 0), stop=(c == CH - 1))
                last.then_inc(ao_ps, 1)

            def transpose_xi(t):
                pe.wait_ge(xi_done, t.count())
                if t.plus(4).exists():
                    pe.wait_ge(xsT_done, t.count(-4))
                for c in range(CH):
                    last = nc.tensor.transpose(ps_x[:, c * P:(c + 1) * P], xi[:, t.c % 2, c * P:(c + 1) * P],
                                               ident)
                last.then_inc(xiT_ps, 1)

            def feed_forward(t):
                pe.wait_ge(xiT_done, t.count())
                if t.has(1):
                    pe.wait_ge(y_done, t.count(1))
                if t.plus(3).exists():
                    pe.wait_ge(s_done, t.count(-3))
                for c in range(CH):
                    last = nc.tensor.matmul(ps_ff, xiT[:, t.c % 2, c, :], ternT[:, c, :],
                                            start=(c == 0), stop=(c == CH - 1))
                last.then_inc(ff_ps, 1)

            run_steps(pe, [(1, transpose_xs), (-2, transpose_p), (1, token_products), (0, scores),
                           (-2, weigh_v), (-3, transpose_xi), (-2, project), (-3, feed_forward),
                           (1, transpose_hn), (1, qkv)])


def position_constants(batch_tokens, tokens, frames):
    import numpy as np

    half = POS // 2
    freqs = np.exp(np.linspace(0.0, float(np.log(1000.0)), half, dtype=np.float32)).astype(np.float32)
    pos = np.arange(tokens, dtype=np.float32) / np.float32(max(1, tokens - 1))
    ang = np.clip(pos, 0.0, 1.0)[:, None] * freqs
    ff = np.concatenate([np.sin(ang), np.cos(ang)], axis=-1).astype(np.float32)
    c = np.zeros((P, C_ALL), np.float32)
    c[:, C_ID:C_ID + P] = np.eye(P, dtype=np.float32)
    count = np.minimum(POOL, frames - np.arange(tokens) * POOL).astype(np.float32)
    for b in range(2):
        c[64 * b:64 * b + tokens, C_INV] = 1.0 / count
        c[0:POS, C_FF + 64 * b:C_FF + 64 * b + tokens] = ff.T
    head = np.arange(P) // 16
    c[:, C_EVEN] = head % 2 == 0
    c[:, C_ODD] = head % 2 == 1
    return c


def kernel(**inputs):
    import numpy as np
    import concourse.bacc as bacc
    from concourse.bass_utils import run_bass_kernel_spmd

    names = ["x", "L0_tok_W", "L0_tok_b", "L0_attn_w_qkv", "L0_attn_b_qkv", "L0_attn_w_out", "L0_attn_b_out",
             "L0_ffn_ternary_weight", "L0_ffn_bias", "L0_ffn_act_scale"]
    rows = {"L0_tok_b", "L0_attn_b_out", "L0_ffn_bias", "L0_ffn_act_scale"}
    B, M, D = np.shape(inputs["x"])
    tokens = -(-M // POOL)
    nc = bacc.Bacc("TRN2", target_bir_lowering=False, num_devices=1)
    arrays, args = {}, []
    for name in names:
        a = np.ascontiguousarray(inputs[name])
        if name in rows:
            a = a.reshape(1, -1)
        arrays[f"in_{name}"] = a
        args.append(nc.dram_tensor(f"in_{name}", a.shape, mybir.dt.from_np(a.dtype), kind="ExternalInput").ap())
    a = position_constants(B, tokens, M)
    arrays["in_consts"] = a
    args.append(nc.dram_tensor("in_consts", a.shape, F32, kind="ExternalInput").ap())
    args.append(nc.dram_tensor("out_0", (B, tokens, D), F32, kind="ExternalOutput").ap())
    audio_tower(nc, *args)
    r = run_bass_kernel_spmd(nc, [arrays], core_ids=[0])
    return r.results[0]["out_0"]
```

```python
from contextlib import ExitStack

import concourse.bass as bass
from concourse import mybir

ALU = mybir.AluOpType
ACT = mybir.ActivationFunctionType
AX = mybir.AxisListType
F32 = mybir.dt.float32
BF16 = mybir.dt.bfloat16
I32 = mybir.dt.int32

P = 128
POOL = 4
POS = 32
HEADS = 16
TOPK_SHARE = 0.1
EPS = 1e-5
ACT_MAX = 127.0
ROUND = 12582912.0
F32_MAX = 3.4028234e38

C_ID, C_INV, C_EVEN, C_ODD, C_FF = 0, P, P + 1, P + 2, P + 3
C_ALL = C_FF + P


def audio_tower(nc, x, w_tok, w_pos, w_qkv, b_qkv, w_out, w_ffn, bias_rows, consts, out):
    B, M, D = x.shape
    N = out.shape[1]
    T = B // 2
    HD = D // HEADS
    PAIRS = HEADS // 2
    TOP = int(TOPK_SHARE * N)
    CH = D // P
    SCALE = float(HD) ** -0.5
    FULL = N - 1 if M < POOL * N else N
    TAIL = M - POOL * FULL
    ROWS = 4
    U = 4
    LAST_LAG = 4
    FIRST_LOOPED = LAST_LAG + 2
    assert D == 2 * P and N == 63 and 2 * HD == 32 and 0 < TOP < 8 and TAIL > 0 and T % 4 == 0

    with ExitStack() as ctx:
        def sb(name, shape, dt=F32):
            return ctx.enter_context(nc.sbuf_tensor(name, shape, dt))

        def sem(name):
            return ctx.enter_context(nc.semaphore(name))

        cst = sb("cst", [P, C_ALL])
        w_tokT = sb("w_tokT", [P, CH, D])
        w_posT = sb("w_posT", [POS + 1, D])
        wqkv = sb("wqkv", [P, CH, 3 * D])
        wo = sb("wo", [P, CH, D])
        tern_i = sb("tern_i", [P, CH, D], I32)
        ternT = sb("ternT", [P, CH, D], BF16)
        rows = sb("rows", [1, 2 * D + 1])
        b_cols = sb("b_cols", [P, 3, CH])
        bv_wide = sb("bv_wide", [P, CH, P])
        bk_par = sb("bk_par", [P, CH, 2])
        ones = sb("ones", [P, P])
        pos_bias = sb("pos_bias", [P, D])
        attn_bias = sb("attn_bias", [P, D])
        ffn_bias = sb("ffn_bias", [P, D])
        scl = sb("scl", [P, 8])
        ident = cst[:, C_ID:C_ID + P]
        X = sb("X", [P, 2, POOL * D])
        xs = sb("xs", [P, 2, D])
        xsT = sb("xsT", [P, 2, CH, P])
        h = sb("h", [P, 2, D])
        hb = sb("hb", [P, 4, D])
        st1 = sb("st1", [P, 2, 6])
        mv1 = sb("mv1", [P, 2, 2])
        rstd1 = sb("rstd1", [P, 2])
        hn = sb("hn", [P, 2, D])
        hnT = sb("hnT", [P, 2, CH, P])
        q = sb("q", [P, 2, CH, P])
        k = sb("k", [P, 2, CH, 2, 2, 64])
        v = sb("v", [P, 4, 2, PAIRS, 2, HD])
        s = sb("s", [P, 2, HEADS, 64])
        top8 = sb("top8", [P, 2, HEADS, 8])
        etop = sb("etop", [P, 2, HEADS, TOP])
        den = sb("den", [P, 2, HEADS])
        lden = sb("lden", [P, 2, HEADS])
        shift = sb("shift", [P, 2, HEADS])
        e = sb("e", [P, 2, HEADS, 64])
        mask = sb("mask", [P, 2, HEADS, 64])
        pr = sb("pr", [P, 2, HEADS, 64])
        prT = sb("prT", [P, 2, PAIRS, P])
        oT = sb("oT", [P, 2, CH, P])
        h2 = sb("h2", [P, 2, D])
        h2b = sb("h2b", [P, 2, D])
        st2 = sb("st2", [P, 2, 6])
        mv2 = sb("mv2", [P, 2, 2])
        rstd2 = sb("rstd2", [P, 2])
        rq = sb("rq", [P, 2])
        qf = sb("qf", [P, 2, D])
        xi = sb("xi", [P, 2, D])
        xiT = sb("xiT", [P, 2, CH, P], BF16)
        y = sb("y", [P, 2, D])
        var_eps = sb("var_eps", [P, 2, 2])
        expo = sb("expo", [P, 1])

        psS = ctx.enter_context(nc.psum_tensor("psS", [P, ROWS, 512], F32))
        psQK = ctx.enter_context(nc.psum_tensor("psQK", [P, 4, P], F32))
        psB = ctx.enter_context(nc.psum_tensor("psB", [P, 3, 512], F32))
        ps_s = psS[:, :, 0:256]
        psT = psS[:, 0:2, :].rearrange("p b (j n) -> p (b j) n", n=P)
        ps_ff = psS[:, 2, 0:256]
        ps_v, ps_n = psB[:, 0, 0:256], psB[:, 0, 256:512]
        ps_x, ps_h = psB[:, 1, 0:256], psB[:, 1, 256:512]
        ps_oT, ps_ao = psB[:, 2, 0:256], psB[:, 2, 256:512]

        consts_in = sem("consts_in")
        pos_w_in = sem("pos_w_in")
        tok_w_in = sem("tok_w_in")
        cols_in = sem("cols_in")
        qkv_w_in = sem("qkv_w_in")
        out_w_in = sem("out_w_in")
        ffn_w_in = sem("ffn_w_in")
        rows_in = sem("rows_in")
        cleared = [sem(f"cleared{i}") for i in range(2)]
        ones_set = sem("ones_set")
        zeroed = sem("zeroed")
        setup_ps = sem("setup_ps")
        setup_sb = sem("setup_sb")
        setup_dve = sem("setup_dve")
        setup_bias = sem("setup_bias")
        x_in = [sem(f"x_in{i}") for i in range(2)]
        half_done = sem("half_done")
        xs_done = sem("xs_done")
        xsT_ps = sem("xsT_ps")
        xsT_done = sem("xsT_done")
        h_ps = sem("h_ps")
        h_done = sem("h_done")
        st1_done = sem("st1_done")
        mv1_done = sem("mv1_done")
        ve1_done = sem("ve1_done")
        rstd1_done = sem("rstd1_done")
        hb_done = sem("hb_done")
        hn_done = sem("hn_done")
        hnT_ps = sem("hnT_ps")
        hnT_done = sem("hnT_done")
        qk_ps = sem("qk_ps")
        v_ps = sem("v_ps")
        qk_done = sem("qk_done")
        v_done = sem("v_done")
        s_ps = sem("s_ps")
        s_done = sem("s_done")
        top8_done = sem("top8_done")
        ztop_done = sem("ztop_done")
        etop_done = sem("etop_done")
        den_done = sem("den_done")
        lden_done = sem("lden_done")
        shift_done = sem("shift_done")
        mask_done = sem("mask_done")
        z_done = sem("z_done")
        e_done = sem("e_done")
        p_done = sem("p_done")
        pT_ps = sem("pT_ps")
        pT_done = sem("pT_done")
        oT_ps = sem("oT_ps")
        oT_done = sem("oT_done")
        ao_ps = sem("ao_ps")
        h2_done = sem("h2_done")
        st2_done = sem("st2_done")
        mv2_done = sem("mv2_done")
        ve2_done = sem("ve2_done")
        rstd2_done = sem("rstd2_done")
        h2b_done = sem("h2b_done")
        rq_done = sem("rq_done")
        qf_done = sem("qf_done")
        xi_done = sem("xi_done")
        xiT_ps = sem("xiT_ps")
        xiT_done = sem("xiT_done")
        ff_ps = sem("ff_ps")
        y_done = sem("y_done")
        y_out = [sem(f"y_out{i}") for i in range(2)]

        x_full = x[:, 0:POOL * FULL, :].rearrange("(t b) (p f) i -> t b p (f i)", b=2, f=POOL)
        x_tail = x[:, POOL * FULL:M, :].rearrange("(t b) f i -> t b (f i)", b=2)
        out_t = out.rearrange("(t b) n o -> t b n o", b=2)

        class Tile:

            def __init__(self, u, c):
                self.u, self.c = u, c

            def plus(self, d):
                return Tile(self.u, self.c + d)

            def exists(self):
                return not isinstance(self.u, int) or 0 <= U * self.u + self.c < T

            def has(self, back):
                return (self.c if not isinstance(self.u, int) else U * self.u + self.c) >= back

            def first(self):
                return isinstance(self.u, int) and self.index() == 0

            def index(self):
                return self.u * U + self.c

            def count(self, back=0, per=1, less=0):
                return self.u * (U * per) + ((self.c - back + 1) * per - less)

            def uses(self, back, per):
                return self.u * (U // 2 * per) + ((self.c - back) // 2 + 1) * per

        def run_steps(eng, stages):
            ahead = max(d for d, _ in stages)
            trips = (T - ahead - FIRST_LOOPED) // U

            def step(n):
                for d, stage in stages:
                    if n.plus(d).exists():
                        stage(n.plus(d))

            for n in range(-ahead, FIRST_LOOPED):
                step(Tile(0, n))
            with eng.Fori(0, trips) as u:
                for n in range(U):
                    step(Tile(u, FIRST_LOOPED + n))
            for n in range(FIRST_LOOPED + trips * U, T + LAST_LAG):
                step(Tile(0, n))

        block = ctx.enter_context(nc.Block())

        @block.sync
        def _(sp):
            def load(t):
                slot = t.c % 2
                if t.has(2):
                    sp.wait_ge(xs_done, t.count(2))
                else:
                    sp.wait_ge(cleared[slot], 1)
                for b in range(2):
                    sp.dma_start(X[64 * b:64 * b + FULL, slot, :], x_full[t.index(), b])\
                        .then_inc(x_in[slot], 16)
                sp.dma_start(X[FULL:P:64, slot, 0:TAIL * D], x_tail[t.index()]).then_inc(x_in[slot], 16)

            def store(t):
                slot = t.c % 2
                sp.wait_ge(y_done, t.count())
                for b in range(2):
                    sp.dma_start(out_t[t.index(), b], y[64 * b:64 * b + N, slot, :])\
                        .then_inc(y_out[slot], 16)

            run_steps(sp, [(5, load), (-4, store)])
            for slot in range(2):
                sp.wait_ge(y_out[slot], 2 * 16 * (T // 2))

        @block.gpsimd
        def _(pool):
            nc.gpsimd.memset(X[:, 0, :], 0.0).then_inc(cleared[0], 1)
            nc.gpsimd.memset(v[:, 0:2, :, :, :, :], 0.0).then_inc(zeroed, 1)
            nc.gpsimd.memset(v[:, 2:4, :, :, :, :], 0.0).then_inc(zeroed, 1)

            def wait_zeros(t):
                if t.first():
                    pool.wait_ge(zeroed, 4)

            def pool_frames(t):
                slot = t.c % 2
                pool.wait_ge(x_in[slot], t.uses(0, 48))
                nc.gpsimd.tensor_tensor(X[:, slot, 0:2 * D], X[:, slot, 0:2 * D], X[:, slot, 2 * D:4 * D],
                                        ALU.add).then_inc(half_done, 1)
                if t.has(2):
                    pool.wait_ge(xsT_ps, t.count(2))
                pool.wait_ge(half_done, t.count())
                nc.gpsimd.tensor_tensor(xs[:, slot, :], X[:, slot, 0:D], X[:, slot, D:2 * D],
                                        ALU.add).then_inc(xs_done, 1)

            def rstd_1(t):
                slot = t.c % 2
                pool.wait_ge(ve1_done, t.count())
                if t.has(2):
                    pool.wait_ge(hn_done, t.count(2))
                nc.gpsimd.tensor_tensor(rstd1[:, slot:slot + 1], var_eps[:, slot, 0:1], expo[:, :],
                                        ALU.pow).then_inc(rstd1_done, 1)

            def residual_1(t):
                if t.first():
                    pool.wait_ge(setup_bias, 1)
                pool.wait_ge(h_done, t.count())
                if t.has(4):
                    pool.wait_ge(h2_done, t.count(4))
                nc.gpsimd.tensor_tensor(hb[:, t.c % 4, :], h[:, t.c % 2, :], attn_bias[:, :],
                                        ALU.add).then_inc(hb_done, 1)

            def subtract_shift(t):
                slot = t.c % 2
                pool.wait_ge(shift_done, t.count())
                pool.wait_ge(s_done, t.count())
                if t.has(2):
                    pool.wait_ge(p_done, t.count(2))
                nc.gpsimd.tensor_tensor(
                    e[:, slot, :, 0:N], s[:, slot, :, 0:N],
                    shift[:, slot, :].unsqueeze(2).broadcast_to([P, HEADS, N]),
                    ALU.subtract).then_inc(z_done, 1)

            def keep_top(t):
                slot = t.c % 2
                pool.wait_ge(e_done, t.count())
                pool.wait_ge(mask_done, t.count())
                if t.has(2):
                    pool.wait_ge(pT_ps, t.count(2, per=2))
                nc.gpsimd.tensor_tensor(pr[:, slot, :, 0:N], e[:, slot, :, 0:N], mask[:, slot, :, 0:N],
                                        ALU.mult).then_inc(p_done, 1)

            def rstd_2(t):
                slot = t.c % 2
                pool.wait_ge(ve2_done, t.count())
                if t.has(2):
                    pool.wait_ge(rq_done, t.count(2))
                nc.gpsimd.tensor_tensor(rstd2[:, slot:slot + 1], var_eps[:, slot, 1:2], expo[:, :],
                                        ALU.pow).then_inc(rstd2_done, 1)

            def residual_2(t):
                slot = t.c % 2
                pool.wait_ge(h2_done, t.count())
                if t.first():
                    pool.wait_ge(setup_bias, 2)
                if t.has(2):
                    pool.wait_ge(y_done, t.count(2))
                nc.gpsimd.tensor_tensor(h2b[:, slot, :], h2[:, slot, :], ffn_bias[:, :],
                                        ALU.add).then_inc(h2b_done, 1)

            run_steps(pool, [(1, wait_zeros), (-1, subtract_shift), (0, residual_1), (1, rstd_1),
                             (-1, keep_top), (-4, residual_2), (3, pool_frames), (-3, rstd_2)])

        @block.scalar
        def _(act):
            act.dma_start(cst[:, :], consts).then_inc(consts_in, 16)
            act.dma_start(w_posT[:, :], w_pos).then_inc(pos_w_in, 16)
            act.dma_start(w_tokT[:, :, :], w_tok.rearrange("(c p) o -> p c o", p=P)).then_inc(tok_w_in, 16)
            act.dma_start(wqkv[:, :, :], w_qkv.rearrange("(c p) o -> p c o", p=P)).then_inc(qkv_w_in, 16)
            act.dma_start(b_cols[:, :, :], b_qkv.rearrange("p (j c) -> p j c", c=CH)).then_inc(cols_in, 16)
            act.dma_start(wo[:, :, :], w_out.rearrange("(c p) o -> p c o", p=P)).then_inc(out_w_in, 16)
            act.dma_start(rows[:, :], bias_rows).then_inc(rows_in, 16)
            act.dma_start(tern_i[:, :, :], w_ffn.rearrange("(c p) o -> p c o", p=P)).then_inc(ffn_w_in, 16)
            nc.scalar.preload_act_table_set("natural_log_exp_and_others")

            def mask_bias(t):
                if not t.first():
                    return
                act.wait_ge(cols_in, 16)
                act.wait_ge(consts_in, 16)
                for c in range(CH):
                    for par in range(2):
                        nc.scalar.activation(bk_par[:, c, par:par + 1], b_cols[:, 1, c:c + 1], ACT.Copy,
                                             scale=cst[:, C_EVEN + par:C_EVEN + par + 1]).then_inc(setup_sb, 1)
                act.wait_ge(setup_sb, 2 * CH)
                act.wait_ge(zeroed, 4)

            def copy_xsT(t):
                slot = t.c % 2
                act.wait_ge(xsT_ps, t.count())
                if t.has(2):
                    act.wait_ge(h_ps, t.count(2))
                nc.scalar.activation(xsT[:, slot, :, :], ps_x.rearrange("p (c n) -> p c n", c=CH),
                                     ACT.Copy).then_inc(xsT_done, 1)

            def copy_hnT(t):
                slot = t.c % 2
                act.wait_ge(hnT_ps, t.count())
                if t.has(2):
                    act.wait_ge(v_ps, t.count(2))
                nc.scalar.activation(hnT[:, slot, :, :], ps_n.rearrange("p (c n) -> p c n", c=CH),
                                     ACT.Copy).then_inc(hnT_done, 1)

            def bias_chunk(t, c):
                slot = t.c % 2
                nc.scalar.activation(q[:, slot, c, :], psQK[:, c, :], ACT.Identity,
                                     bias=b_cols[:, 0, c:c + 1])
                for par in range(2):
                    last = nc.scalar.activation(
                        k[:, slot, c, :, par, :], psQK[:, CH + c, :].rearrange("p (b n) -> p b n", b=2),
                        ACT.Identity, bias=bk_par[:, c, par:par + 1],
                        scale=cst[:, C_EVEN + par:C_EVEN + par + 1])
                last.then_inc(qk_done, 1)

            def bias_qk_0(t):
                act.wait_ge(qk_ps, t.count())
                if t.has(2):
                    act.wait_ge(s_ps, t.count(2))
                bias_chunk(t, 0)

            def bias_qk_1(t):
                bias_chunk(t, 1)

            def copy_v(t):
                slot = t.c % 4
                act.wait_ge(v_ps, t.count())
                if t.has(4):
                    act.wait_ge(oT_ps, t.count(4))
                for par in range(2):
                    last = nc.scalar.activation(
                        v[64 * par:64 * par + 64, slot, :, :, par, :].rearrange("p b j d -> p (b j) d"),
                        ps_v[64 * par:64 * par + 64, :].rearrange("p (j d) -> p j d", d=HD), ACT.Copy)
                last.then_inc(v_done, 1)

            def copy_s(t):
                slot = t.c % 2
                act.wait_ge(s_ps, t.count())
                if t.has(2):
                    act.wait_ge(z_done, t.count(2))
                    act.wait_ge(mask_done, t.count(2))
                nc.scalar.activation(s[:, slot, :, :].rearrange("p (r g) n -> p r (g n)", r=ROWS), ps_s,
                                     ACT.Copy).then_inc(s_done, 1)

            def exp_top(t):
                slot = t.c % 2
                act.wait_ge(ztop_done, t.count())
                nc.scalar.activation(etop[:, slot, :, :], etop[:, slot, :, :], ACT.Exp,
                                     scale=SCALE).then_inc(etop_done, 1)

            def log_den(t):
                slot = t.c % 2
                act.wait_ge(den_done, t.count())
                if t.has(2):
                    act.wait_ge(shift_done, t.count(2))
                nc.scalar.activation(lden[:, slot, :], den[:, slot, :], ACT.Ln).then_inc(lden_done, 1)

            def exp_all(t):
                slot = t.c % 2
                act.wait_ge(z_done, t.count())
                nc.scalar.activation(e[:, slot, :, 0:N], e[:, slot, :, 0:N], ACT.Exp,
                                     scale=SCALE).then_inc(e_done, 1)

            def copy_pT(t):
                slot = t.c % 2
                if t.has(2):
                    act.wait_ge(oT_ps, t.count(2))
                for i in range(2):
                    act.wait_ge(pT_ps, t.count(per=2, less=1 - i))
                    nc.scalar.activation(prT[:, slot, 4 * i:4 * i + 4, :], psT[:, 4 * i:4 * i + 4, :],
                                         ACT.Copy).then_inc(pT_done, 1)

            def copy_oT(t):
                slot = t.c % 2
                act.wait_ge(oT_ps, t.count())
                if t.has(2):
                    act.wait_ge(ao_ps, t.count(2))
                nc.scalar.activation(oT[:, slot, :, :], ps_oT.rearrange("p (c n) -> p c n", c=CH),
                                     ACT.Copy).then_inc(oT_done, 1)

            run_steps(act, [(-1, exp_all), (0, copy_s), (2, copy_xsT), (1, copy_hnT), (-2, copy_pT),
                            (0, exp_top), (1, mask_bias), (1, bias_qk_0), (0, log_den), (1, bias_qk_1),
                            (-2, copy_oT), (1, copy_v)])

        @block.vector
        def _(dve):
            nc.vector.memset(X[:, 1, :], 0.0).then_inc(cleared[1], 1)
            nc.vector.memset(ones[:, :], 1.0).then_inc(ones_set, 1)
            nc.vector.memset(expo[:, :], -0.5).then_inc(zeroed, 1)
            nc.vector.memset(pr[:, :, :, :], 0.0).then_inc(zeroed, 1)
            inv_scale, scale_back = scl[:, 3:4], scl[:, 4:5]

            def token_bias(t):
                if not t.first():
                    return
                dve.wait_ge(setup_ps, 1)
                nc.vector.tensor_copy(pos_bias[:, :], ps_ao).then_inc(setup_dve, 1)
                dve.wait_ge(setup_dve, 1)

            def attention_bias(t):
                if not t.first():
                    return
                dve.wait_ge(cols_in, 16)
                dve.wait_ge(ones_set, 1)
                for c in range(CH):
                    nc.vector.tensor_scalar(bv_wide[:, c, :], ones[:, :], b_cols[:, 2, c:c + 1], None,
                                            ALU.mult).then_inc(setup_dve, 1)
                dve.wait_ge(setup_ps, 2)
                nc.vector.tensor_copy(attn_bias[:, :], ps_oT).then_inc(setup_bias, 1)
                dve.wait_ge(setup_ps, 3)
                nc.vector.tensor_copy(ffn_bias[:, :], ps_n).then_inc(setup_bias, 1)
                nc.vector.tensor_copy(scl[:, 0:1], ps_v[:, 0:1]).then_inc(setup_bias, 1)

            def ffn_constants(t):
                if not t.first():
                    return
                dve.wait_ge(ffn_w_in, 16)
                nc.vector.tensor_scalar(ternT[:, :, :], tern_i[:, :, :], -1.0, None, ALU.add).then_inc(setup_bias, 1)
                dve.wait_ge(setup_bias, 4)
                nc.vector.tensor_scalar(scl[:, 1:2], scl[:, 0:1], EPS, F32_MAX, ALU.max, ALU.min).then_inc(setup_bias, 1)
                nc.vector.tensor_tensor(scl[:, 2:3], scl[:, 0:1], scl[:, 0:1], ALU.is_equal).then_inc(setup_bias, 1)
                dve.wait_ge(setup_bias, 6)
                nc.vector.reciprocal(scl[:, 3:4], scl[:, 1:2]).then_inc(setup_bias, 1)
                nc.vector.tensor_tensor(scl[:, 4:5], scl[:, 1:2], scl[:, 2:3], ALU.mult).then_inc(setup_bias, 1)
                dve.wait_ge(setup_bias, 8)

            def sum_top(t):
                slot = t.c % 2
                dve.wait_ge(etop_done, t.count())
                if t.has(2):
                    dve.wait_ge(lden_done, t.count(2))
                nc.vector.tensor_reduce(den[:, slot, :], etop[:, slot, :, :], AX.X, ALU.add)\
                    .then_inc(den_done, 1)

            def make_shift(t):
                slot = t.c % 2
                dve.wait_ge(lden_done, t.count())
                if t.has(2):
                    dve.wait_ge(z_done, t.count(2))
                nc.vector.scalar_tensor_tensor(
                    out=shift[:, slot, :], in0=lden[:, slot, :], scalar=1.0 / SCALE,
                    in1=top8[:, slot, :, 0], op0=ALU.mult, op1=ALU.add).then_inc(shift_done, 1)

            def mask_top(t):
                slot = t.c % 2
                dve.wait_ge(s_done, t.count())
                dve.wait_ge(top8_done, t.count(per=2))
                if t.has(2):
                    dve.wait_ge(p_done, t.count(2))
                nc.vector.tensor_tensor(
                    mask[:, slot, :, 0:N], s[:, slot, :, 0:N],
                    top8[:, slot, :, TOP - 1:TOP].broadcast_to([P, HEADS, N]),
                    ALU.is_ge).then_inc(mask_done, 1)

            def tokens(t):
                slot = t.c % 2
                dve.wait_ge(h_ps, t.count())
                if t.has(2):
                    dve.wait_ge(hb_done, t.count(2))
                nc.vector.scalar_tensor_tensor(
                    out=h[:, slot, :], in0=ps_h, scalar=cst[:, C_INV:C_INV + 1], in1=pos_bias[:, :],
                    op0=ALU.mult, op1=ALU.add).then_inc(h_done, 1)

            def statistics_1(t):
                slot = t.c % 2
                dve.wait_ge(h_done, t.count())
                nc.vector.bn_stats(out=st1[:, slot, :], in_=h[:, slot, :]).then_inc(st1_done, 1)

            def moments_1(t):
                slot = t.c % 2
                dve.wait_ge(st1_done, t.count())
                dve.nop(nofuse=True)
                nc.vector.bn_aggr(out=mv1[:, slot, :], in_=st1[:, slot, :]).then_inc(mv1_done, 1)

            def variance_1(t):
                slot = t.c % 2
                dve.wait_ge(mv1_done, t.count())
                if t.has(2):
                    dve.wait_ge(rstd1_done, t.count(2))
                nc.vector.tensor_scalar(var_eps[:, slot, 0:1], mv1[:, slot, 1:2], EPS, None,
                                        ALU.add).then_inc(ve1_done, 1)

            def normalise(t):
                slot = t.c % 2
                dve.wait_ge(rstd1_done, t.count())
                if t.has(2):
                    dve.wait_ge(hnT_ps, t.count(2))
                nc.vector.tensor_scalar(hn[:, slot, :], h[:, slot, :], mv1[:, slot, 0:1],
                                        rstd1[:, slot:slot + 1], ALU.subtract, ALU.mult).then_inc(hn_done, 1)

            def attended(t):
                slot = t.c % 2
                dve.wait_ge(ao_ps, t.count())
                dve.wait_ge(hb_done, t.count())
                if t.has(2):
                    dve.wait_ge(h2b_done, t.count(2))
                nc.vector.tensor_tensor(h2[:, slot, :], ps_ao, hb[:, t.c % 4, :], ALU.add)\
                    .then_inc(h2_done, 1)

            def statistics_2(t):
                slot = t.c % 2
                dve.wait_ge(h2_done, t.count())
                nc.vector.bn_stats(out=st2[:, slot, :], in_=h2[:, slot, :]).then_inc(st2_done, 1)

            def moments_2(t):
                slot = t.c % 2
                dve.wait_ge(st2_done, t.count())
                dve.nop(nofuse=True)
                nc.vector.bn_aggr(out=mv2[:, slot, :], in_=st2[:, slot, :]).then_inc(mv2_done, 1)

            def variance_2(t):
                slot = t.c % 2
                dve.wait_ge(mv2_done, t.count())
                if t.has(2):
                    dve.wait_ge(rstd2_done, t.count(2))
                nc.vector.tensor_scalar(var_eps[:, slot, 1:2], mv2[:, slot, 1:2], EPS, None,
                                        ALU.add).then_inc(ve2_done, 1)

            def quant_scale(t):
                slot = t.c % 2
                dve.wait_ge(rstd2_done, t.count())
                nc.vector.tensor_tensor(rq[:, slot:slot + 1], rstd2[:, slot:slot + 1], inv_scale,
                                        ALU.mult).then_inc(rq_done, 1)

            def scaled(t):
                slot = t.c % 2
                dve.wait_ge(rq_done, t.count())
                nc.vector.tensor_scalar(qf[:, slot, :], h2[:, slot, :], mv2[:, slot, 0:1],
                                        rq[:, slot:slot + 1], ALU.subtract, ALU.mult).then_inc(qf_done, 1)

            def rounded(t):
                slot = t.c % 2
                dve.wait_ge(qf_done, t.count())
                if t.has(2):
                    dve.wait_ge(xiT_ps, t.count(2))
                nc.vector.tensor_scalar(xi[:, slot, :], qf[:, slot, :], ACT_MAX, ROUND, ALU.min, ALU.add)\
                    .then_inc(xi_done, 1)

            def integers(t):
                slot = t.c % 2
                dve.wait_ge(xiT_ps, t.count())
                if t.has(2):
                    dve.wait_ge(ff_ps, t.count(2))
                nc.vector.tensor_scalar(xiT[:, slot, :, :], ps_x.rearrange("p (c n) -> p c n", c=CH),
                                        ROUND - ACT_MAX, ROUND, ALU.max, ALU.subtract).then_inc(xiT_done, 1)

            def top_half(t, i):
                for g in range(i * HEADS // 2, (i + 1) * HEADS // 2):
                    last = nc.vector.max(out=top8[:, t.c % 2, g, :], in_=s[:, t.c % 2, g, 0:N])
                last.then_inc(top8_done, 1)

            def top_scores_0(t):
                dve.wait_ge(s_done, t.count())
                if t.has(2):
                    dve.wait_ge(shift_done, t.count(2))
                    dve.wait_ge(mask_done, t.count(2))
                dve.nop(nofuse=True)
                top_half(t, 0)

            def top_scores_1(t):
                top_half(t, 1)

            def shift_top(t):
                slot = t.c % 2
                dve.wait_ge(top8_done, t.count(per=2))
                if t.has(2):
                    dve.wait_ge(den_done, t.count(2))
                nc.vector.tensor_tensor(
                    etop[:, slot, :, :], top8[:, slot, :, 0:TOP],
                    top8[:, slot, :, 0:1].broadcast_to([P, HEADS, TOP]),
                    ALU.subtract).then_inc(ztop_done, 1)

            def finished(t):
                slot = t.c % 2
                dve.wait_ge(ff_ps, t.count())
                dve.wait_ge(h2b_done, t.count())
                if t.has(2):
                    dve.wait_ge(y_out[slot], t.uses(2, 32))
                nc.vector.scalar_tensor_tensor(
                    out=y[:, slot, :], in0=ps_ff, scalar=scale_back, in1=h2b[:, slot, :],
                    op0=ALU.mult, op1=ALU.add).then_inc(y_done, 1)

            run_steps(dve, [(0, attention_bias), (-4, quant_scale), (-4, scaled), (-4, rounded), (1, token_bias),
                            (1, tokens), (1, statistics_1), (1, moments_1), (1, variance_1),
                            (-4, integers), (1, normalise), (0, top_scores_0), (-3, attended),
                            (0, top_scores_1), (0, shift_top), (-3, statistics_2), (0, sum_top), (-3, moments_2),
                            (-4, finished), (-3, variance_2),
                            (0, make_shift), (0, mask_top), (0, ffn_constants)])

        @block.tensor
        def _(pe):
            pe.wait_ge(consts_in, 16)
            pe.wait_ge(pos_w_in, 16)
            nc.tensor.matmul(ps_ao, cst[0:POS + 1, C_FF:C_FF + P], w_posT[:, :], start=True, stop=True)\
                .then_inc(setup_ps, 1)

            def attention_bias(t):
                if not t.first():
                    return
                pe.wait_ge(out_w_in, 16)
                pe.wait_ge(rows_in, 16)
                pe.wait_ge(setup_dve, 1 + CH)
                for c in range(CH):
                    nc.tensor.matmul(ps_oT, bv_wide[:, c, :], wo[:, c, :], start=(c == 0), stop=False)
                nc.tensor.matmul(ps_oT, ones[0:1, :], rows[0:1, 0:D], start=False, stop=True).then_inc(setup_ps, 1)
                pe.wait_ge(hnT_done, t.count())
                pe.wait_ge(v_done, t.count())
                nc.tensor.matmul(ps_n, ones[0:1, :], rows[0:1, D:2 * D], start=True, stop=True)
                nc.tensor.matmul(ps_v[:, 0:1], ones[0:1, :], rows[0:1, 2 * D:2 * D + 1], start=True, stop=True)\
                    .then_inc(setup_ps, 1)
                pe.wait_ge(setup_bias, 3)

            def weights_in(t):
                if t.first():
                    pe.wait_ge(qkv_w_in, 16)

            def transpose_xs(t):
                pe.wait_ge(xs_done, t.count())
                if t.has(6):
                    pe.wait_ge(xiT_done, t.count(6))
                if t.has(1):
                    pe.wait_ge(h_done, t.count(1))
                for c in range(CH):
                    last = nc.tensor.transpose(ps_x[:, c * P:(c + 1) * P], xs[:, t.c % 2, c * P:(c + 1) * P],
                                               ident)
                last.then_inc(xsT_ps, 1)

            def token_products(t):
                pe.wait_ge(xsT_done, t.count())
                if t.first():
                    pe.wait_ge(tok_w_in, 16)
                for c in range(CH):
                    last = nc.tensor.matmul(ps_h, xsT[:, t.c % 2, c, :], w_tokT[:, c, :],
                                            start=(c == 0), stop=(c == CH - 1))
                last.then_inc(h_ps, 1)

            def transpose_hn(t):
                pe.wait_ge(hn_done, t.count())
                if t.has(1):
                    pe.wait_ge(v_done, t.count(1))
                for c in range(CH):
                    last = nc.tensor.transpose(ps_n[:, c * P:(c + 1) * P], hn[:, t.c % 2, c * P:(c + 1) * P],
                                               ident)
                last.then_inc(hnT_ps, 1)

            def queries_keys(t):
                slot = t.c % 2
                pe.wait_ge(hnT_done, t.count())
                for o in range(2 * CH):
                    for c in range(CH):
                        last = nc.tensor.matmul(psQK[:, o, :], wqkv[:, c, o * P:(o + 1) * P],
                                                hnT[:, slot, c, :], start=(c == 0), stop=(c == CH - 1))
                last.then_inc(qk_ps, 1)

            def values(t):
                slot = t.c % 2
                for b in range(2):
                    for c in range(CH):
                        for par in range(2):
                            w = wqkv[:, c, 2 * D:3 * D].rearrange("p (j a d) -> p a j d", a=2, d=HD)[:, par]
                            last = nc.tensor.matmul(
                                ps_v[64 * par:64 * par + 64, b * P:(b + 1) * P],
                                hnT[:, slot, c, 64 * b:64 * b + 64], w, start=(c == 0), stop=(c == CH - 1))
                last.then_inc(v_ps, 1)

            def score_chunk(t, c):
                slot = t.c % 2
                pe.wait_ge(qk_done, t.count(per=CH, less=CH - 1 - c))
                for r in range(ROWS):
                    at = slice(32 * r, 32 * r + 32)
                    for b in range(2):
                        last = nc.tensor.matmul(
                            ps_s[64 * b:64 * b + 64, r, c * P:(c + 1) * P],
                            q[at, slot, c, 64 * b:64 * b + 64],
                            k[at, slot, c, b, :, :].rearrange("p a n -> p (a n)"), start=True, stop=True)
                return last

            def scores_0(t):
                if t.has(1):
                    pe.wait_ge(s_done, t.count(1))
                if t.has(3):
                    pe.wait_ge(pT_done, t.count(3, per=2))
                if t.has(5):
                    pe.wait_ge(y_done, t.count(5))
                score_chunk(t, 0)

            def scores_1(t):
                score_chunk(t, 1).then_inc(s_ps, 1)

            def transpose_p(t):
                pe.wait_ge(p_done, t.count())
                if t.plus(2).exists():
                    pe.wait_ge(s_done, t.count(-2))
                for i in range(2):
                    for j in range(4 * i, 4 * i + 4):
                        last = nc.tensor.transpose(
                            psT[:, j, :], pr[:, t.c % 2, 2 * j:2 * j + 2, :].rearrange("p a n -> p (a n)"), ident)
                    last.then_inc(pT_ps, 1)

            def weigh_v(t):
                slot = t.c % 2
                pe.wait_ge(v_done, t.count())
                if t.has(1):
                    pe.wait_ge(h2_done, t.count(1))
                pe.wait_ge(pT_done, t.count(per=2))
                for c in range(CH):
                    for b in range(2):
                        for r in range(ROWS):
                            last = nc.tensor.matmul(
                                ps_oT[32 * r:32 * r + 32, c * P + 64 * b:c * P + 64 * b + 64],
                                v[:, t.c % 4, b, ROWS * c + r, :, :].rearrange("p a d -> p (a d)"),
                                prT[:, slot, 2 * r + c, 64 * b:64 * b + 64], start=True, stop=True)
                last.then_inc(oT_ps, 1)

            def project(t):
                pe.wait_ge(oT_done, t.count())
                for c in range(CH):
                    last = nc.tensor.matmul(ps_ao, oT[:, t.c % 2, c, :], wo[:, c, :],
                                            start=(c == 0), stop=(c == CH - 1))
                last.then_inc(ao_ps, 1)

            def transpose_xi(t):
                pe.wait_ge(xi_done, t.count())
                if t.plus(5).exists():
                    pe.wait_ge(xsT_done, t.count(-5))
                    pe.wait_ge(h_done, t.count(-5))
                for c in range(CH):
                    last = nc.tensor.transpose(ps_x[:, c * P:(c + 1) * P], xi[:, t.c % 2, c * P:(c + 1) * P],
                                               ident)
                last.then_inc(xiT_ps, 1)

            def feed_forward(t):
                pe.wait_ge(xiT_done, t.count())
                if t.has(1):
                    pe.wait_ge(y_done, t.count(1))
                if t.plus(4).exists():
                    pe.wait_ge(s_done, t.count(-4))
                for c in range(CH):
                    last = nc.tensor.matmul(ps_ff, xiT[:, t.c % 2, c, :], ternT[:, c, :],
                                            start=(c == 0), stop=(c == CH - 1))
                last.then_inc(ff_ps, 1)

            run_steps(pe, [(0, attention_bias), (0, scores_0), (1, token_products), (0, scores_1),
                           (-4, transpose_xi), (-3, project), (2, transpose_xs), (-4, feed_forward),
                           (1, transpose_hn), (-2, transpose_p), (1, weights_in), (1, queries_keys),
                           (-2, weigh_v), (1, values)])


def position_constants(tokens, frames):
    import numpy as np

    half = POS // 2
    freqs = np.exp(np.linspace(0.0, float(np.log(1000.0)), half, dtype=np.float32)).astype(np.float32)
    pos = np.arange(tokens, dtype=np.float32) / np.float32(max(1, tokens - 1))
    ang = np.clip(pos, 0.0, 1.0)[:, None] * freqs
    ff = np.concatenate([np.sin(ang), np.cos(ang)], axis=-1).astype(np.float32)
    c = np.zeros((P, C_ALL), np.float32)
    c[:, C_ID:C_ID + P] = np.eye(P, dtype=np.float32)
    count = np.minimum(POOL, frames - np.arange(tokens) * POOL).astype(np.float32)
    for b in range(2):
        c[64 * b:64 * b + tokens, C_INV] = 1.0 / count
        c[0:POS, C_FF + 64 * b:C_FF + 64 * b + tokens] = ff.T
    head = np.arange(P) // 16
    c[POS, C_FF:C_FF + P] = 1.0
    c[:, C_EVEN] = head % 2 == 0
    c[:, C_ODD] = head % 2 == 1
    return c


def kernel(**inputs):
    import numpy as np
    import concourse.bacc as bacc
    from concourse.bass_utils import run_bass_kernel_spmd

    B, M, D = np.shape(inputs["x"])
    tokens = -(-M // POOL)
    w_tok = np.asarray(inputs["L0_tok_W"]).T
    row = [np.asarray(inputs[n]).reshape(1, -1) for n in ("L0_attn_b_out", "L0_ffn_bias", "L0_ffn_act_scale")]
    laid_out = {
        "x": inputs["x"],
        "w_tok": w_tok[:D],
        "w_pos": np.concatenate([w_tok[D:], np.asarray(inputs["L0_tok_b"]).reshape(1, -1)]),
        "w_qkv": inputs["L0_attn_w_qkv"],
        "b_qkv": np.asarray(inputs["L0_attn_b_qkv"]).reshape(-1, P).T,
        "w_out": inputs["L0_attn_w_out"],
        "w_ffn": np.asarray(inputs["L0_ffn_ternary_weight"]).T,
        "bias_rows": np.concatenate(row, axis=1),
        "consts": position_constants(tokens, M),
    }
    nc = bacc.Bacc("TRN2", target_bir_lowering=False, num_devices=1)
    arrays, args = {}, []
    for name, a in laid_out.items():
        a = np.ascontiguousarray(a)
        arrays[f"in_{name}"] = a
        args.append(nc.dram_tensor(f"in_{name}", a.shape, mybir.dt.from_np(a.dtype), kind="ExternalInput").ap())
    args.append(nc.dram_tensor("out_0", (B, tokens, D), F32, kind="ExternalOutput").ap())
    audio_tower(nc, *args)
    r = run_bass_kernel_spmd(nc, [arrays], core_ids=[0])
    return r.results[0]["out_0"]
```

```python
from contextlib import ExitStack

import concourse.bass as bass
from concourse import mybir

ALU = mybir.AluOpType
ACT = mybir.ActivationFunctionType
AX = mybir.AxisListType
F32 = mybir.dt.float32
BF16 = mybir.dt.bfloat16
I32 = mybir.dt.int32

P = 128
POOL = 4
POS = 32
HEADS = 16
TOPK_SHARE = 0.1
EPS = 1e-5
ACT_MAX = 127.0
ROUND = 12582912.0
F32_MAX = 3.4028234e38

C_ID, C_INV, C_EVEN, C_ODD, C_FF = 0, P, P + 1, P + 2, P + 3
C_ALL = C_FF + P


def audio_tower(nc, x, w_tok, w_pos, w_qkv, columns, w_out, b_out, w_ffn, b_ffn, consts, out):
    B, M, D = x.shape
    N = out.shape[1]
    T = B // 2
    HD = D // HEADS
    PAIRS = HEADS // 2
    TOP = int(TOPK_SHARE * N)
    CH = D // P
    SCALE = float(HD) ** -0.5
    FULL = N - 1 if M < POOL * N else N
    TAIL = M - POOL * FULL
    ROWS = 4
    U = 4
    LAST_LAG = 4
    FILLED = 3
    FIRST_LOOPED = LAST_LAG + 2
    assert D == 2 * P and N == 63 and 2 * HD == 32 and 0 < TOP < 8 and TAIL > 0 and T % 4 == 0

    with ExitStack() as ctx:
        def sb(name, shape, dt=F32):
            return ctx.enter_context(nc.sbuf_tensor(name, shape, dt))

        def sem(name):
            return ctx.enter_context(nc.semaphore(name))

        cst = sb("cst", [P, C_ALL])
        w_tokT = sb("w_tokT", [P, CH, D])
        w_posT = sb("w_posT", [POS + 1, D])
        wqkv = sb("wqkv", [P, CH, 3 * D])
        wo = sb("wo", [P, CH, D])
        tern_i = sb("tern_i", [P, CH, D], I32)
        ternT = sb("ternT", [P, CH, D], BF16)
        b_out_row = sb("b_out_row", [1, D])
        b_cols = sb("b_cols", [P, 3 * CH + 1])
        bv_wide = sb("bv_wide", [P, CH, P])
        bk_par = sb("bk_par", [P, CH, 2])
        ones = sb("ones", [P, P])
        pos_bias = sb("pos_bias", [P, D])
        attn_bias = sb("attn_bias", [P, D])
        ffn_bias = sb("ffn_bias", [P, D])
        scl = sb("scl", [P, 8])
        ident = cst[:, C_ID:C_ID + P]
        X = sb("X", [P, 2, POOL * D])
        xs = sb("xs", [P, 2, D])
        xsT = sb("xsT", [P, 2, CH, P])
        h = sb("h", [P, 2, D])
        hb = sb("hb", [P, 4, D])
        st1 = sb("st1", [P, 2, 6])
        mv1 = sb("mv1", [P, 2, 2])
        rstd1 = sb("rstd1", [P, 2])
        hn = sb("hn", [P, 2, D])
        hnT = sb("hnT", [P, 2, CH, P])
        q = sb("q", [P, 2, CH, P])
        k = sb("k", [P, 2, CH, 2, 2, 64])
        v = sb("v", [P, 4, 2, PAIRS, 2, HD])
        s = sb("s", [P, 2, HEADS, 64])
        top8 = sb("top8", [P, 2, HEADS, 8])
        etop = sb("etop", [P, 2, HEADS, TOP])
        den = sb("den", [P, 2, HEADS])
        lden = sb("lden", [P, 2, HEADS])
        shift = sb("shift", [P, 2, HEADS])
        e = sb("e", [P, 2, HEADS, 64])
        mask = sb("mask", [P, 2, HEADS, 64])
        pr = sb("pr", [P, 2, HEADS, 64])
        prT = sb("prT", [P, 2, PAIRS, P])
        oT = sb("oT", [P, 2, CH, P])
        h2 = sb("h2", [P, 2, D])
        h2b = sb("h2b", [P, 2, D])
        st2 = sb("st2", [P, 2, 6])
        mv2 = sb("mv2", [P, 2, 2])
        rstd2 = sb("rstd2", [P, 2])
        rq = sb("rq", [P, 2])
        qf = sb("qf", [P, 2, D])
        xi = sb("xi", [P, 2, D])
        xiT = sb("xiT", [P, 2, CH, P], BF16)
        y = sb("y", [P, 2, D])
        var_eps = sb("var_eps", [P, 2, 2])
        expo = sb("expo", [P, 1])

        psS = ctx.enter_context(nc.psum_tensor("psS", [P, ROWS, 512], F32))
        psQK = ctx.enter_context(nc.psum_tensor("psQK", [P, 4, P], F32))
        psB = ctx.enter_context(nc.psum_tensor("psB", [P, 3, 512], F32))
        ps_s = psS[:, :, 0:256]
        psT = psS[:, 0:2, :].rearrange("p b (j n) -> p (b j) n", n=P)
        ps_ff = psS[:, 2, 0:256]
        ps_v, ps_n = psB[:, 0, 0:256], psB[:, 0, 256:512]
        ps_x, ps_h = psB[:, 1, 0:256], psB[:, 1, 256:512]
        ps_oT, ps_ao = psB[:, 2, 0:256], psB[:, 2, 256:512]

        consts_in = sem("consts_in")
        pos_w_in = sem("pos_w_in")
        tok_w_in = sem("tok_w_in")
        cols_in = sem("cols_in")
        qkv_w_in = sem("qkv_w_in")
        out_w_in = sem("out_w_in")
        ffn_w_in = sem("ffn_w_in")
        b_out_in = sem("b_out_in")
        ffn_bias_in = sem("ffn_bias_in")
        cleared = [sem(f"cleared{i}") for i in range(2)]
        ones_done = sem("ones_done")
        zeroed = sem("zeroed")
        pos_bias_ps = sem("pos_bias_ps")
        pos_bias_done = sem("pos_bias_done")
        bk_par_done = sem("bk_par_done")
        spread_done = sem("spread_done")
        attn_bias_ps = sem("attn_bias_ps")
        attn_bias_done = sem("attn_bias_done")
        ternT_done = sem("ternT_done")
        clamp_done = sem("clamp_done")
        scale_done = sem("scale_done")
        x_in = [sem(f"x_in{i}") for i in range(2)]
        half_done = sem("half_done")
        xs_done = sem("xs_done")
        xsT_ps = sem("xsT_ps")
        xsT_done = sem("xsT_done")
        h_ps = sem("h_ps")
        h_done = sem("h_done")
        st1_done = sem("st1_done")
        mv1_done = sem("mv1_done")
        ve1_done = sem("ve1_done")
        rstd1_done = sem("rstd1_done")
        hb_done = sem("hb_done")
        hn_done = sem("hn_done")
        hnT_ps = sem("hnT_ps")
        hnT_done = sem("hnT_done")
        qk_ps = sem("qk_ps")
        v_ps = sem("v_ps")
        qk_done = sem("qk_done")
        v_done = sem("v_done")
        s_ps = sem("s_ps")
        s_done = sem("s_done")
        top8_done = sem("top8_done")
        ztop_done = sem("ztop_done")
        etop_done = sem("etop_done")
        den_done = sem("den_done")
        lden_done = sem("lden_done")
        shift_done = sem("shift_done")
        mask_done = sem("mask_done")
        z_done = sem("z_done")
        e_done = sem("e_done")
        p_done = sem("p_done")
        pT_ps = sem("pT_ps")
        pT_done = sem("pT_done")
        oT_ps = sem("oT_ps")
        oT_done = sem("oT_done")
        ao_ps = sem("ao_ps")
        h2_done = sem("h2_done")
        st2_done = sem("st2_done")
        mv2_done = sem("mv2_done")
        ve2_done = sem("ve2_done")
        rstd2_done = sem("rstd2_done")
        h2b_done = sem("h2b_done")
        rq_done = sem("rq_done")
        qf_done = sem("qf_done")
        xi_done = sem("xi_done")
        xiT_ps = sem("xiT_ps")
        xiT_done = sem("xiT_done")
        ff_ps = sem("ff_ps")
        y_done = sem("y_done")
        y_out = [sem(f"y_out{i}") for i in range(2)]

        x_full = x[:, 0:POOL * FULL, :].rearrange("(t b) (p f) i -> t b p (f i)", b=2, f=POOL)
        x_tail = x[:, POOL * FULL:M, :].rearrange("(t b) f i -> t b (f i)", b=2)
        out_t = out.rearrange("(t b) n o -> t b n o", b=2)

        class Tile:

            def __init__(self, u, c):
                self.u, self.c = u, c

            def plus(self, d):
                return Tile(self.u, self.c + d)

            def exists(self):
                return not isinstance(self.u, int) or 0 <= U * self.u + self.c < T

            def has(self, back):
                return (self.c if not isinstance(self.u, int) else U * self.u + self.c) >= back

            def first(self):
                return isinstance(self.u, int) and self.index() == 0

            def index(self):
                return self.u * U + self.c

            def count(self, back=0, per=1, less=0):
                return self.u * (U * per) + ((self.c - back + 1) * per - less)

            def uses(self, back, per):
                return self.u * (U // 2 * per) + ((self.c - back) // 2 + 1) * per

        def run_steps(eng, stages, fill=None, drain=None):
            ahead = max(d for d, _ in stages)
            trips = (T - ahead - FIRST_LOOPED) // U

            def step(n, order):
                for d, stage in order:
                    if n.plus(d).exists():
                        stage(n.plus(d))

            for n in range(-ahead, FIRST_LOOPED):
                step(Tile(0, n), fill if fill and n < FILLED else stages)
            with eng.Fori(0, trips) as u:
                for n in range(U):
                    step(Tile(u, FIRST_LOOPED + n), stages)
            for n in range(FIRST_LOOPED + trips * U, T + LAST_LAG):
                step(Tile(0, n), drain if drain and n >= T else stages)

        block = ctx.enter_context(nc.Block())

        @block.sync
        def _(sp):
            def load(t):
                slot = t.c % 2
                if t.has(2):
                    sp.wait_ge(xs_done, t.count(2))
                else:
                    sp.wait_ge(cleared[slot], 1)
                for b in range(2):
                    sp.dma_start(X[64 * b:64 * b + FULL, slot, :], x_full[t.index(), b])\
                        .then_inc(x_in[slot], 16)
                sp.dma_start(X[FULL:P:64, slot, 0:TAIL * D], x_tail[t.index()]).then_inc(x_in[slot], 16)

            def store(t):
                slot = t.c % 2
                sp.wait_ge(y_done, t.count())
                for b in range(2):
                    sp.dma_start(out_t[t.index(), b], y[64 * b:64 * b + N, slot, :])\
                        .then_inc(y_out[slot], 16)

            run_steps(sp, [(5, load), (-4, store)])
            for slot in range(2):
                sp.wait_ge(y_out[slot], 2 * 16 * (T // 2))

        @block.gpsimd
        def _(pool):
            nc.gpsimd.memset(X[:, 0, :], 0.0).then_inc(cleared[0], 1)
            nc.gpsimd.memset(v[:, 0:2, :, :, :, :], 0.0).then_inc(zeroed, 1)
            nc.gpsimd.memset(v[:, 2:4, :, :, :, :], 0.0).then_inc(zeroed, 1)

            def wait_zeros(t):
                if t.first():
                    pool.wait_ge(zeroed, 4)

            def pool_frames(t):
                slot = t.c % 2
                pool.wait_ge(x_in[slot], t.uses(0, 48))
                nc.gpsimd.tensor_tensor(X[:, slot, 0:2 * D], X[:, slot, 0:2 * D], X[:, slot, 2 * D:4 * D],
                                        ALU.add).then_inc(half_done, 1)
                if t.has(2):
                    pool.wait_ge(xsT_ps, t.count(2))
                pool.wait_ge(half_done, t.count())
                nc.gpsimd.tensor_tensor(xs[:, slot, :], X[:, slot, 0:D], X[:, slot, D:2 * D],
                                        ALU.add).then_inc(xs_done, 1)

            def rstd_1(t):
                slot = t.c % 2
                pool.wait_ge(ve1_done, t.count())
                if t.has(2):
                    pool.wait_ge(hn_done, t.count(2))
                nc.gpsimd.tensor_tensor(rstd1[:, slot:slot + 1], var_eps[:, slot, 0:1], expo[:, :],
                                        ALU.pow).then_inc(rstd1_done, 1)

            def residual_1(t):
                if t.first():
                    pool.wait_ge(attn_bias_done, 1)
                pool.wait_ge(h_done, t.count())
                if t.has(4):
                    pool.wait_ge(h2_done, t.count(4))
                nc.gpsimd.tensor_tensor(hb[:, t.c % 4, :], h[:, t.c % 2, :], attn_bias[:, :],
                                        ALU.add).then_inc(hb_done, 1)

            def subtract_shift(t):
                slot = t.c % 2
                pool.wait_ge(shift_done, t.count())
                pool.wait_ge(s_done, t.count())
                if t.has(2):
                    pool.wait_ge(p_done, t.count(2))
                nc.gpsimd.tensor_tensor(
                    e[:, slot, :, 0:N], s[:, slot, :, 0:N],
                    shift[:, slot, :].unsqueeze(2).broadcast_to([P, HEADS, N]),
                    ALU.subtract).then_inc(z_done, 1)

            def keep_top(t):
                slot = t.c % 2
                pool.wait_ge(e_done, t.count())
                pool.wait_ge(mask_done, t.count())
                if t.has(2):
                    pool.wait_ge(pT_ps, t.count(2, per=2))
                nc.gpsimd.tensor_tensor(pr[:, slot, :, 0:N], e[:, slot, :, 0:N], mask[:, slot, :, 0:N],
                                        ALU.mult).then_inc(p_done, 1)

            def rstd_2(t):
                slot = t.c % 2
                pool.wait_ge(ve2_done, t.count())
                if t.has(2):
                    pool.wait_ge(rq_done, t.count(2))
                nc.gpsimd.tensor_tensor(rstd2[:, slot:slot + 1], var_eps[:, slot, 1:2], expo[:, :],
                                        ALU.pow).then_inc(rstd2_done, 1)

            def residual_2(t):
                slot = t.c % 2
                pool.wait_ge(h2_done, t.count())
                if t.first():
                    pool.wait_ge(ffn_bias_in, 16)
                if t.has(2):
                    pool.wait_ge(y_done, t.count(2))
                nc.gpsimd.tensor_tensor(h2b[:, slot, :], h2[:, slot, :], ffn_bias[:, :],
                                        ALU.add).then_inc(h2b_done, 1)

            run_steps(pool, [(-1, subtract_shift), (0, residual_1), (1, rstd_1), (-1, keep_top),
                             (-4, residual_2), (3, pool_frames), (-3, rstd_2)],
                      fill=[(1, wait_zeros), (1, rstd_1), (-1, subtract_shift), (0, residual_1),
                            (3, pool_frames), (-1, keep_top)],
                      drain=[(-1, subtract_shift), (-1, keep_top), (-4, residual_2), (-3, rstd_2)])

        @block.scalar
        def _(act):
            act.dma_start(cst[:, :], consts).then_inc(consts_in, 16)
            act.dma_start(w_posT[:, :], w_pos).then_inc(pos_w_in, 16)
            act.dma_start(w_tokT[:, :, :], w_tok.rearrange("(c p) o -> p c o", p=P)).then_inc(tok_w_in, 16)
            act.dma_start(b_cols[:, :], columns).then_inc(cols_in, 16)
            act.dma_start(wqkv[:, :, :], w_qkv.rearrange("(c p) o -> p c o", p=P)).then_inc(qkv_w_in, 16)
            nc.scalar.preload_act_table_set("natural_log_exp_and_others")
            act.dma_start(wo[:, :, :], w_out.rearrange("(c p) o -> p c o", p=P)).then_inc(out_w_in, 16)
            act.dma_start(b_out_row[:, :], b_out).then_inc(b_out_in, 16)
            act.dma_start(ffn_bias[:, :], b_ffn.broadcast_to([P, D])).then_inc(ffn_bias_in, 16)
            act.dma_start(tern_i[:, :, :], w_ffn.rearrange("(c p) o -> p c o", p=P)).then_inc(ffn_w_in, 16)

            def mask_bias(t):
                if not t.first():
                    return
                act.wait_ge(cols_in, 16)
                act.wait_ge(consts_in, 16)
                for c in range(CH):
                    for par in range(2):
                        nc.scalar.activation(bk_par[:, c, par:par + 1], b_cols[:, CH + c:CH + c + 1], ACT.Copy,
                                             scale=cst[:, C_EVEN + par:C_EVEN + par + 1]).then_inc(bk_par_done, 1)
                act.wait_ge(bk_par_done, 2 * CH)
                act.wait_ge(zeroed, 4)

            def copy_xsT(t):
                slot = t.c % 2
                act.wait_ge(xsT_ps, t.count())
                if t.has(2):
                    act.wait_ge(h_ps, t.count(2))
                nc.scalar.activation(xsT[:, slot, :, :], ps_x.rearrange("p (c n) -> p c n", c=CH),
                                     ACT.Copy).then_inc(xsT_done, 1)

            def copy_hnT(t):
                slot = t.c % 2
                act.wait_ge(hnT_ps, t.count())
                if t.has(2):
                    act.wait_ge(v_ps, t.count(2))
                nc.scalar.activation(hnT[:, slot, :, :], ps_n.rearrange("p (c n) -> p c n", c=CH),
                                     ACT.Copy).then_inc(hnT_done, 1)

            def bias_chunk(t, c):
                slot = t.c % 2
                nc.scalar.activation(q[:, slot, c, :], psQK[:, c, :], ACT.Identity,
                                     bias=b_cols[:, c:c + 1])
                for par in range(2):
                    last = nc.scalar.activation(
                        k[:, slot, c, :, par, :], psQK[:, CH + c, :].rearrange("p (b n) -> p b n", b=2),
                        ACT.Identity, bias=bk_par[:, c, par:par + 1],
                        scale=cst[:, C_EVEN + par:C_EVEN + par + 1])
                last.then_inc(qk_done, 1)

            def bias_qk_0(t):
                act.wait_ge(qk_ps, t.count())
                if t.has(2):
                    act.wait_ge(s_ps, t.count(2))
                bias_chunk(t, 0)

            def bias_qk_1(t):
                bias_chunk(t, 1)

            def copy_v(t):
                slot = t.c % 4
                act.wait_ge(v_ps, t.count())
                if t.has(4):
                    act.wait_ge(oT_ps, t.count(4))
                for par in range(2):
                    last = nc.scalar.activation(
                        v[64 * par:64 * par + 64, slot, :, :, par, :].rearrange("p b j d -> p (b j) d"),
                        ps_v[64 * par:64 * par + 64, :].rearrange("p (j d) -> p j d", d=HD), ACT.Copy)
                last.then_inc(v_done, 1)

            def copy_s(t):
                slot = t.c % 2
                act.wait_ge(s_ps, t.count())
                if t.has(2):
                    act.wait_ge(z_done, t.count(2))
                    act.wait_ge(mask_done, t.count(2))
                nc.scalar.activation(s[:, slot, :, :].rearrange("p (r g) n -> p r (g n)", r=ROWS), ps_s,
                                     ACT.Copy).then_inc(s_done, 1)

            def exp_top(t):
                slot = t.c % 2
                act.wait_ge(ztop_done, t.count())
                nc.scalar.activation(etop[:, slot, :, :], etop[:, slot, :, :], ACT.Exp,
                                     scale=SCALE).then_inc(etop_done, 1)

            def log_den(t):
                slot = t.c % 2
                act.wait_ge(den_done, t.count())
                if t.has(2):
                    act.wait_ge(shift_done, t.count(2))
                nc.scalar.activation(lden[:, slot, :], den[:, slot, :], ACT.Ln).then_inc(lden_done, 1)

            def exp_all(t):
                slot = t.c % 2
                act.wait_ge(z_done, t.count())
                nc.scalar.activation(e[:, slot, :, 0:N], e[:, slot, :, 0:N], ACT.Exp,
                                     scale=SCALE).then_inc(e_done, 1)

            def copy_pT(t):
                slot = t.c % 2
                if t.has(2):
                    act.wait_ge(oT_ps, t.count(2))
                for i in range(2):
                    act.wait_ge(pT_ps, t.count(per=2, less=1 - i))
                    nc.scalar.activation(prT[:, slot, 4 * i:4 * i + 4, :], psT[:, 4 * i:4 * i + 4, :],
                                         ACT.Copy).then_inc(pT_done, 1)

            def copy_oT(t):
                slot = t.c % 2
                act.wait_ge(oT_ps, t.count())
                if t.has(2):
                    act.wait_ge(ao_ps, t.count(2))
                nc.scalar.activation(oT[:, slot, :, :], ps_oT.rearrange("p (c n) -> p c n", c=CH),
                                     ACT.Copy).then_inc(oT_done, 1)

            run_steps(act, [(-1, exp_all), (0, copy_s), (2, copy_xsT), (1, copy_hnT), (-2, copy_pT),
                            (0, exp_top), (1, bias_qk_0), (0, log_den), (1, bias_qk_1),
                            (-2, copy_oT), (1, copy_v)],
                      fill=[(1, copy_hnT), (0, copy_s), (2, copy_xsT), (1, mask_bias), (-1, exp_all),
                            (1, bias_qk_0), (0, exp_top), (-2, copy_pT), (1, bias_qk_1), (0, log_den),
                            (1, copy_v), (-2, copy_oT)],
                      drain=[(-2, copy_pT), (-1, exp_all), (-2, copy_oT)])

        @block.vector
        def _(dve):
            nc.vector.memset(X[:, 1, :], 0.0).then_inc(cleared[1], 1)
            nc.vector.memset(ones[:, :], 1.0).then_inc(ones_done, 1)
            nc.vector.memset(expo[:, :], -0.5).then_inc(zeroed, 1)
            nc.vector.memset(pr[:, :, :, :], 0.0).then_inc(zeroed, 1)
            act_scale = b_cols[:, 3 * CH:3 * CH + 1]
            inv_scale, scale_back = scl[:, 3:4], scl[:, 4:5]

            def token_bias(t):
                if not t.first():
                    return
                dve.wait_ge(pos_bias_ps, 1)
                nc.vector.tensor_copy(pos_bias[:, :], ps_ao).then_inc(pos_bias_done, 1)
                dve.wait_ge(pos_bias_done, 1)

            def spread_bias(t):
                if not t.first():
                    return
                dve.wait_ge(cols_in, 16)
                dve.wait_ge(ones_done, 1)
                for c in range(CH):
                    nc.vector.tensor_scalar(bv_wide[:, c, :], ones[:, :], b_cols[:, 2 * CH + c:2 * CH + c + 1],
                                            None, ALU.mult).then_inc(spread_done, 1)

            def attention_bias(t):
                if not t.first():
                    return
                dve.wait_ge(attn_bias_ps, 1)
                nc.vector.tensor_copy(attn_bias[:, :], ps_oT).then_inc(attn_bias_done, 1)

            def ffn_constants(t):
                if not t.first():
                    return
                dve.wait_ge(ffn_w_in, 16)
                nc.vector.tensor_scalar(ternT[:, :, :], tern_i[:, :, :], -1.0, None, ALU.add)\
                    .then_inc(ternT_done, 1)
                nc.vector.tensor_scalar(scl[:, 1:2], act_scale, EPS, F32_MAX, ALU.max, ALU.min)\
                    .then_inc(clamp_done, 1)
                nc.vector.tensor_tensor(scl[:, 2:3], act_scale, act_scale, ALU.is_equal).then_inc(clamp_done, 1)
                dve.wait_ge(clamp_done, 2)
                nc.vector.reciprocal(scl[:, 3:4], scl[:, 1:2]).then_inc(scale_done, 1)
                nc.vector.tensor_tensor(scl[:, 4:5], scl[:, 1:2], scl[:, 2:3], ALU.mult).then_inc(scale_done, 1)
                dve.wait_ge(scale_done, 2)

            def sum_top(t):
                slot = t.c % 2
                dve.wait_ge(etop_done, t.count())
                if t.has(2):
                    dve.wait_ge(lden_done, t.count(2))
                nc.vector.tensor_reduce(den[:, slot, :], etop[:, slot, :, :], AX.X, ALU.add)\
                    .then_inc(den_done, 1)

            def make_shift(t):
                slot = t.c % 2
                dve.wait_ge(lden_done, t.count())
                if t.has(2):
                    dve.wait_ge(z_done, t.count(2))
                nc.vector.scalar_tensor_tensor(
                    out=shift[:, slot, :], in0=lden[:, slot, :], scalar=1.0 / SCALE,
                    in1=top8[:, slot, :, 0], op0=ALU.mult, op1=ALU.add).then_inc(shift_done, 1)

            def mask_top(t):
                slot = t.c % 2
                dve.wait_ge(s_done, t.count())
                dve.wait_ge(top8_done, t.count(per=2))
                if t.has(2):
                    dve.wait_ge(p_done, t.count(2))
                nc.vector.tensor_tensor(
                    mask[:, slot, :, 0:N], s[:, slot, :, 0:N],
                    top8[:, slot, :, TOP - 1:TOP].broadcast_to([P, HEADS, N]),
                    ALU.is_ge).then_inc(mask_done, 1)

            def tokens(t):
                slot = t.c % 2
                dve.wait_ge(h_ps, t.count())
                if t.has(2):
                    dve.wait_ge(hb_done, t.count(2))
                nc.vector.scalar_tensor_tensor(
                    out=h[:, slot, :], in0=ps_h, scalar=cst[:, C_INV:C_INV + 1], in1=pos_bias[:, :],
                    op0=ALU.mult, op1=ALU.add).then_inc(h_done, 1)

            def statistics_1(t):
                slot = t.c % 2
                dve.wait_ge(h_done, t.count())
                nc.vector.bn_stats(out=st1[:, slot, :], in_=h[:, slot, :]).then_inc(st1_done, 1)

            def moments_1(t):
                slot = t.c % 2
                dve.wait_ge(st1_done, t.count())
                dve.nop(nofuse=True)
                nc.vector.bn_aggr(out=mv1[:, slot, :], in_=st1[:, slot, :]).then_inc(mv1_done, 1)

            def variance_1(t):
                slot = t.c % 2
                dve.wait_ge(mv1_done, t.count())
                if t.has(2):
                    dve.wait_ge(rstd1_done, t.count(2))
                nc.vector.tensor_scalar(var_eps[:, slot, 0:1], mv1[:, slot, 1:2], EPS, None,
                                        ALU.add).then_inc(ve1_done, 1)

            def normalise(t):
                slot = t.c % 2
                dve.wait_ge(rstd1_done, t.count())
                if t.has(2):
                    dve.wait_ge(hnT_ps, t.count(2))
                nc.vector.tensor_scalar(hn[:, slot, :], h[:, slot, :], mv1[:, slot, 0:1],
                                        rstd1[:, slot:slot + 1], ALU.subtract, ALU.mult).then_inc(hn_done, 1)

            def attended(t):
                slot = t.c % 2
                dve.wait_ge(ao_ps, t.count())
                dve.wait_ge(hb_done, t.count())
                if t.has(2):
                    dve.wait_ge(h2b_done, t.count(2))
                nc.vector.tensor_tensor(h2[:, slot, :], ps_ao, hb[:, t.c % 4, :], ALU.add)\
                    .then_inc(h2_done, 1)

            def statistics_2(t):
                slot = t.c % 2
                dve.wait_ge(h2_done, t.count())
                nc.vector.bn_stats(out=st2[:, slot, :], in_=h2[:, slot, :]).then_inc(st2_done, 1)

            def moments_2(t):
                slot = t.c % 2
                dve.wait_ge(st2_done, t.count())
                dve.nop(nofuse=True)
                nc.vector.bn_aggr(out=mv2[:, slot, :], in_=st2[:, slot, :]).then_inc(mv2_done, 1)

            def variance_2(t):
                slot = t.c % 2
                dve.wait_ge(mv2_done, t.count())
                if t.has(2):
                    dve.wait_ge(rstd2_done, t.count(2))
                nc.vector.tensor_scalar(var_eps[:, slot, 1:2], mv2[:, slot, 1:2], EPS, None,
                                        ALU.add).then_inc(ve2_done, 1)

            def quant_scale(t):
                slot = t.c % 2
                dve.wait_ge(rstd2_done, t.count())
                nc.vector.tensor_tensor(rq[:, slot:slot + 1], rstd2[:, slot:slot + 1], inv_scale,
                                        ALU.mult).then_inc(rq_done, 1)

            def scaled(t):
                slot = t.c % 2
                dve.wait_ge(rq_done, t.count())
                nc.vector.tensor_scalar(qf[:, slot, :], h2[:, slot, :], mv2[:, slot, 0:1],
                                        rq[:, slot:slot + 1], ALU.subtract, ALU.mult).then_inc(qf_done, 1)

            def rounded(t):
                slot = t.c % 2
                dve.wait_ge(qf_done, t.count())
                if t.has(2):
                    dve.wait_ge(xiT_ps, t.count(2))
                nc.vector.tensor_scalar(xi[:, slot, :], qf[:, slot, :], ACT_MAX, ROUND, ALU.min, ALU.add)\
                    .then_inc(xi_done, 1)

            def integers(t):
                slot = t.c % 2
                dve.wait_ge(xiT_ps, t.count())
                if t.has(2):
                    dve.wait_ge(ff_ps, t.count(2))
                nc.vector.tensor_scalar(xiT[:, slot, :, :], ps_x.rearrange("p (c n) -> p c n", c=CH),
                                        ROUND - ACT_MAX, ROUND, ALU.max, ALU.subtract).then_inc(xiT_done, 1)

            def top_half(t, i):
                for g in range(i * HEADS // 2, (i + 1) * HEADS // 2):
                    last = nc.vector.max(out=top8[:, t.c % 2, g, :], in_=s[:, t.c % 2, g, 0:N])
                last.then_inc(top8_done, 1)

            def top_scores_0(t):
                dve.wait_ge(s_done, t.count())
                if t.has(2):
                    dve.wait_ge(shift_done, t.count(2))
                    dve.wait_ge(mask_done, t.count(2))
                dve.nop(nofuse=True)
                top_half(t, 0)

            def top_scores_1(t):
                top_half(t, 1)

            def shift_top(t):
                slot = t.c % 2
                dve.wait_ge(top8_done, t.count(per=2))
                if t.has(2):
                    dve.wait_ge(den_done, t.count(2))
                nc.vector.tensor_tensor(
                    etop[:, slot, :, :], top8[:, slot, :, 0:TOP],
                    top8[:, slot, :, 0:1].broadcast_to([P, HEADS, TOP]),
                    ALU.subtract).then_inc(ztop_done, 1)

            def finished(t):
                slot = t.c % 2
                dve.wait_ge(ff_ps, t.count())
                dve.wait_ge(h2b_done, t.count())
                if t.has(2):
                    dve.wait_ge(y_out[slot], t.uses(2, 32))
                nc.vector.scalar_tensor_tensor(
                    out=y[:, slot, :], in0=ps_ff, scalar=scale_back, in1=h2b[:, slot, :],
                    op0=ALU.mult, op1=ALU.add).then_inc(y_done, 1)

            run_steps(dve, [(-1, mask_top), (-4, quant_scale), (-4, scaled), (-4, rounded),
                            (1, tokens), (1, statistics_1), (1, moments_1), (1, variance_1),
                            (-4, integers), (1, normalise), (-3, attended), (0, top_scores_0),
                            (0, top_scores_1), (0, shift_top), (-3, statistics_2), (0, sum_top),
                            (-3, moments_2), (-4, finished), (-3, variance_2), (0, make_shift)],
                      fill=[(1, token_bias), (1, spread_bias), (1, tokens), (1, statistics_1),
                            (1, moments_1), (1, variance_1), (1, normalise), (-1, mask_top), (1, attention_bias),
                            (0, ffn_constants), (0, top_scores_0), (0, top_scores_1), (0, shift_top),
                            (0, sum_top), (0, make_shift)],
                      drain=[(-1, mask_top), (-4, quant_scale), (-4, scaled), (-4, rounded), (-3, attended),
                             (-3, statistics_2), (-4, integers), (-3, moments_2), (-3, variance_2),
                             (-4, finished)])

        @block.tensor
        def _(pe):
            pe.wait_ge(consts_in, 16)
            pe.wait_ge(pos_w_in, 16)
            nc.tensor.matmul(ps_ao, cst[0:POS + 1, C_FF:C_FF + P], w_posT[:, :], start=True, stop=True)\
                .then_inc(pos_bias_ps, 1)

            def attention_bias(t):
                if not t.first():
                    return
                pe.wait_ge(out_w_in, 16)
                pe.wait_ge(b_out_in, 16)
                pe.wait_ge(spread_done, CH)
                pe.wait_ge(pos_bias_done, 1)
                for c in range(CH):
                    nc.tensor.matmul(ps_oT, bv_wide[:, c, :], wo[:, c, :], start=(c == 0), stop=False)
                nc.tensor.matmul(ps_oT, ones[0:1, :], b_out_row[:, :], start=False, stop=True)\
                    .then_inc(attn_bias_ps, 1)

            def weights_in(t):
                if t.first():
                    pe.wait_ge(qkv_w_in, 16)

            def transpose_xs(t):
                pe.wait_ge(xs_done, t.count())
                if t.has(6):
                    pe.wait_ge(xiT_done, t.count(6))
                if t.has(1):
                    pe.wait_ge(h_done, t.count(1))
                for c in range(CH):
                    last = nc.tensor.transpose(ps_x[:, c * P:(c + 1) * P], xs[:, t.c % 2, c * P:(c + 1) * P],
                                               ident)
                last.then_inc(xsT_ps, 1)

            def token_products(t):
                pe.wait_ge(xsT_done, t.count())
                if t.first():
                    pe.wait_ge(tok_w_in, 16)
                for c in range(CH):
                    last = nc.tensor.matmul(ps_h, xsT[:, t.c % 2, c, :], w_tokT[:, c, :],
                                            start=(c == 0), stop=(c == CH - 1))
                last.then_inc(h_ps, 1)

            def transpose_hn(t):
                pe.wait_ge(hn_done, t.count())
                if t.has(1):
                    pe.wait_ge(v_done, t.count(1))
                for c in range(CH):
                    last = nc.tensor.transpose(ps_n[:, c * P:(c + 1) * P], hn[:, t.c % 2, c * P:(c + 1) * P],
                                               ident)
                last.then_inc(hnT_ps, 1)

            def queries_keys(t):
                slot = t.c % 2
                pe.wait_ge(hnT_done, t.count())
                for o in range(2 * CH):
                    for c in range(CH):
                        last = nc.tensor.matmul(psQK[:, o, :], wqkv[:, c, o * P:(o + 1) * P],
                                                hnT[:, slot, c, :], start=(c == 0), stop=(c == CH - 1))
                last.then_inc(qk_ps, 1)

            def values(t):
                slot = t.c % 2
                for b in range(2):
                    for c in range(CH):
                        for par in range(2):
                            w = wqkv[:, c, 2 * D:3 * D].rearrange("p (j a d) -> p a j d", a=2, d=HD)[:, par]
                            last = nc.tensor.matmul(
                                ps_v[64 * par:64 * par + 64, b * P:(b + 1) * P],
                                hnT[:, slot, c, 64 * b:64 * b + 64], w, start=(c == 0), stop=(c == CH - 1))
                last.then_inc(v_ps, 1)

            def score_chunk(t, c):
                slot = t.c % 2
                pe.wait_ge(qk_done, t.count(per=CH, less=CH - 1 - c))
                for r in range(ROWS):
                    at = slice(32 * r, 32 * r + 32)
                    for b in range(2):
                        last = nc.tensor.matmul(
                            ps_s[64 * b:64 * b + 64, r, c * P:(c + 1) * P],
                            q[at, slot, c, 64 * b:64 * b + 64],
                            k[at, slot, c, b, :, :].rearrange("p a n -> p (a n)"), start=True, stop=True)
                return last

            def scores_0(t):
                if t.has(1):
                    pe.wait_ge(s_done, t.count(1))
                if t.has(3):
                    pe.wait_ge(pT_done, t.count(3, per=2))
                if t.has(5):
                    pe.wait_ge(y_done, t.count(5))
                score_chunk(t, 0)

            def scores_1(t):
                score_chunk(t, 1).then_inc(s_ps, 1)

            def transpose_p(t):
                pe.wait_ge(p_done, t.count())
                if t.plus(2).exists():
                    pe.wait_ge(s_done, t.count(-2))
                for i in range(2):
                    for j in range(4 * i, 4 * i + 4):
                        last = nc.tensor.transpose(
                            psT[:, j, :], pr[:, t.c % 2, 2 * j:2 * j + 2, :].rearrange("p a n -> p (a n)"), ident)
                    last.then_inc(pT_ps, 1)

            def weigh_v(t):
                slot = t.c % 2
                pe.wait_ge(v_done, t.count())
                if t.first():
                    pe.wait_ge(attn_bias_done, 1)
                if t.has(1):
                    pe.wait_ge(h2_done, t.count(1))
                pe.wait_ge(pT_done, t.count(per=2))
                for c in range(CH):
                    for b in range(2):
                        for r in range(ROWS):
                            last = nc.tensor.matmul(
                                ps_oT[32 * r:32 * r + 32, c * P + 64 * b:c * P + 64 * b + 64],
                                v[:, t.c % 4, b, ROWS * c + r, :, :].rearrange("p a d -> p (a d)"),
                                prT[:, slot, 2 * r + c, 64 * b:64 * b + 64], start=True, stop=True)
                last.then_inc(oT_ps, 1)

            def project(t):
                pe.wait_ge(oT_done, t.count())
                for c in range(CH):
                    last = nc.tensor.matmul(ps_ao, oT[:, t.c % 2, c, :], wo[:, c, :],
                                            start=(c == 0), stop=(c == CH - 1))
                last.then_inc(ao_ps, 1)

            def transpose_xi(t):
                pe.wait_ge(xi_done, t.count())
                if t.plus(5).exists():
                    pe.wait_ge(xsT_done, t.count(-5))
                    pe.wait_ge(h_done, t.count(-5))
                for c in range(CH):
                    last = nc.tensor.transpose(ps_x[:, c * P:(c + 1) * P], xi[:, t.c % 2, c * P:(c + 1) * P],
                                               ident)
                last.then_inc(xiT_ps, 1)

            def feed_forward(t):
                if t.first():
                    pe.wait_ge(ternT_done, 1)
                pe.wait_ge(xiT_done, t.count())
                if t.has(1):
                    pe.wait_ge(y_done, t.count(1))
                if t.plus(4).exists():
                    pe.wait_ge(s_done, t.count(-4))
                for c in range(CH):
                    last = nc.tensor.matmul(ps_ff, xiT[:, t.c % 2, c, :], ternT[:, c, :],
                                            start=(c == 0), stop=(c == CH - 1))
                last.then_inc(ff_ps, 1)

            run_steps(pe, [(1, token_products), (0, scores_0), (0, scores_1), (-4, transpose_xi),
                           (-3, project), (2, transpose_xs), (-4, feed_forward), (1, transpose_hn),
                           (-2, transpose_p), (1, queries_keys), (-2, weigh_v), (1, values)],
                      fill=[(1, token_products), (0, scores_0), (0, scores_1), (1, attention_bias),
                            (1, transpose_hn), (2, transpose_xs), (1, weights_in), (1, queries_keys),
                            (-2, transpose_p), (1, values), (-2, weigh_v)],
                      drain=[(-3, project), (-2, transpose_p), (-4, transpose_xi), (-2, weigh_v),
                             (-4, feed_forward)])


def position_constants(tokens, frames):
    import numpy as np

    half = POS // 2
    freqs = np.exp(np.linspace(0.0, float(np.log(1000.0)), half, dtype=np.float32)).astype(np.float32)
    pos = np.arange(tokens, dtype=np.float32) / np.float32(max(1, tokens - 1))
    ang = np.clip(pos, 0.0, 1.0)[:, None] * freqs
    ff = np.concatenate([np.sin(ang), np.cos(ang)], axis=-1).astype(np.float32)
    c = np.zeros((P, C_ALL), np.float32)
    c[:, C_ID:C_ID + P] = np.eye(P, dtype=np.float32)
    count = np.minimum(POOL, frames - np.arange(tokens) * POOL).astype(np.float32)
    for b in range(2):
        c[64 * b:64 * b + tokens, C_INV] = 1.0 / count
        c[0:POS, C_FF + 64 * b:C_FF + 64 * b + tokens] = ff.T
    head = np.arange(P) // 16
    c[POS, C_FF:C_FF + P] = 1.0
    c[:, C_EVEN] = head % 2 == 0
    c[:, C_ODD] = head % 2 == 1
    return c


def kernel(**inputs):
    import numpy as np
    import concourse.bacc as bacc
    from concourse.bass_utils import run_bass_kernel_spmd

    B, M, D = np.shape(inputs["x"])
    tokens = -(-M // POOL)
    w_tok = np.asarray(inputs["L0_tok_W"]).T
    by_channel = np.asarray(inputs["L0_attn_b_qkv"]).reshape(-1, P).T
    scale = np.broadcast_to(np.asarray(inputs["L0_ffn_act_scale"]).reshape(1, 1), (P, 1))
    laid_out = {
        "x": inputs["x"],
        "w_tok": w_tok[:D],
        "w_pos": np.concatenate([w_tok[D:], np.asarray(inputs["L0_tok_b"]).reshape(1, -1)]),
        "w_qkv": inputs["L0_attn_w_qkv"],
        "columns": np.concatenate([by_channel, scale], axis=1),
        "w_out": inputs["L0_attn_w_out"],
        "b_out": np.asarray(inputs["L0_attn_b_out"]).reshape(1, -1),
        "w_ffn": np.asarray(inputs["L0_ffn_ternary_weight"]).T,
        "b_ffn": np.asarray(inputs["L0_ffn_bias"]).reshape(1, -1),
        "consts": position_constants(tokens, M),
    }
    nc = bacc.Bacc("TRN2", target_bir_lowering=False, num_devices=1)
    arrays, args = {}, []
    for name, a in laid_out.items():
        a = np.ascontiguousarray(a)
        arrays[f"in_{name}"] = a
        args.append(nc.dram_tensor(f"in_{name}", a.shape, mybir.dt.from_np(a.dtype), kind="ExternalInput").ap())
    args.append(nc.dram_tensor("out_0", (B, tokens, D), F32, kind="ExternalOutput").ap())
    audio_tower(nc, *args)
    r = run_bass_kernel_spmd(nc, [arrays], core_ids=[0])
    return r.results[0]["out_0"]
```
